# Optimizing a Trainium2 kernel written in Bass

```python
import numpy as np
import jax
import jax.numpy as jnp

def _softmax(x, axis=-1):
    return jax.nn.softmax(x, axis=axis)
def _gelu(x):
    return jax.nn.gelu(x, approximate=True)
def _silu(x):
    return jax.nn.silu(x)
def _sigmoid(x):
    return jax.nn.sigmoid(x)
def _layernorm(x, axis=-1, eps=1e-5):
    m = jnp.mean(x, axis=axis, keepdims=True)
    v = jnp.var(x, axis=axis, keepdims=True)
    return (x - m) / jnp.sqrt(v + eps)
def _scatter_add(tgt, idx, src, axis=0):
    return tgt.at[idx].add(src)
def _segment_sum(src, seg, n):
    return jax.ops.segment_sum(src, seg, n)

kernel_name = 'mk_adj_preln_d2_adj_256_403b32'

def setup_inputs(seed: int = 0):
    np.random.seed(seed)
    _w = jnp.asarray
    def _rec_inputs():
        import jax
        import jax.numpy as jnp
        _gk = jax.random.key(seed)
        x = -0.0005146 + 1 * jax.random.normal(jax.random.fold_in(_gk, 1), (8, 2048, 256), jnp.float32)
        _a = jax.random.bernoulli(jax.random.fold_in(_gk, 2), 0.015625, (8, 2048, 2048))
        _a = jnp.logical_or(_a, jnp.swapaxes(_a, -1, -2))
        _a = jnp.logical_or(_a, jnp.eye(2048, dtype=bool))
        adj = _a.astype(jnp.int32)
        return x, adj
    x, adj = _rec_inputs()
    def _L0_gnn_setup():
        import jax, jax.numpy as jnp
        import numpy as np
        B, N, C, OUT, S = (4, 2048, 256, 256, 25)
        DENSITY = 0.008
        key = jax.random.key(seed)
        kA, kX, kW = jax.random.split(key, 3)
        A = jax.random.bernoulli(kA, DENSITY, (B, N, N)).astype(jnp.int32)
        X = jax.random.normal(kX, (B, N, C), dtype=jnp.float32)
        W = jax.random.normal(kW, (2 * C, OUT), dtype=jnp.float32) * np.float32(1.0 / np.sqrt(2 * C))
        b = jnp.zeros((OUT,), dtype=jnp.float32)
        return {'A': A, 'X': X, 'W': W, 'b': b}
    _L0_gnn_all = _L0_gnn_setup()
    _L0_gnn_in = {k: v for k, v in _L0_gnn_all.items() if k in ('W', 'b', )}
    del _L0_gnn_all

    def _L1_gnn_setup():
        import jax, jax.numpy as jnp
        import numpy as np
        NEG_INF = -1000000000000.0
        ALPHA = 0.2
        key = jax.random.key(seed)
        k1, k2, k3, k4, k5 = jax.random.split(key, 5)
        B, N, Cin, Cout = (8, 2048, 256, 256)
        x = jax.random.normal(k1, (B, N, Cin), dtype=jnp.float32)
        mask = jax.random.randint(k2, (B, N, N), 0, 2, dtype=jnp.int32)
        W = jax.random.normal(k3, (Cout, Cin), dtype=jnp.float32) * Cin ** (-0.5)
        a = jax.random.normal(k4, (2, Cout), dtype=jnp.float32) * Cout ** (-0.5)
        bias = jax.random.normal(k5, (Cout,), dtype=jnp.float32)
        return {'x': x, 'mask': mask, 'W': W, 'a': a, 'bias': bias}
    _L1_gnn_all = _L1_gnn_setup()
    _L1_gnn_in = {k: v for k, v in _L1_gnn_all.items() if k in ('W', 'a', 'bias', )}
    del _L1_gnn_all

    return {
        "x": x,
        "adj": adj,
        "L0_gnn_W": _L0_gnn_in["W"],
        "L0_gnn_b": _L0_gnn_in["b"],
        "L1_gnn_W": _L1_gnn_in["W"],
        "L1_gnn_a": _L1_gnn_in["a"],
        "L1_gnn_bias": _L1_gnn_in["bias"],
    }

def reference(x, adj, L0_gnn_W, L0_gnn_b, L1_gnn_W, L1_gnn_a, L1_gnn_bias):
    import jax
    import jax.numpy as jnp
    def _L0_gnn_ref(A, X, W, b):
        import jax, jax.numpy as jnp
        import numpy as np
        B, N, C, OUT, S = (4, 2048, 256, 256, 25)
        DENSITY = 0.008
        mask = A != 0
        neg_inf = jnp.float32(-jnp.inf)
        pri = -jnp.arange(N, dtype=jnp.float32)
        scores = jnp.where(mask, pri, neg_inf)
        vals, idx = jax.lax.top_k(scores, S)
        valid = vals > neg_inf
        feats = jax.vmap(lambda x, i: x[i])(X, idx)
        feats = jnp.where(valid[..., None], feats, neg_inf)
        agg = feats.max(axis=2)
        degree = mask.sum(axis=-1)
        agg = jnp.where((degree <= S)[..., None], jnp.maximum(agg, 0.0), agg)
        h = jnp.concatenate([X, agg], axis=-1)
        out = jax.nn.relu(jnp.einsum('bnf,fo->bno', h, W) + b)
        return out

    def _L1_gnn_ref(x, mask, W, a, bias):
        import jax, jax.numpy as jnp
        import numpy as np
        NEG_INF = -1000000000000.0
        ALPHA = 0.2
        hidden = jnp.einsum('bni,oi->bno', x, W)
        av = jnp.einsum('bno,ko->bnk', hidden, a)
        attn1, attn2 = (av[..., 0], av[..., 1])
        attn = attn1[:, :, None] + attn2[:, None, :]
        attn = jax.nn.leaky_relu(attn, negative_slope=ALPHA)
        attn = jnp.where(mask > 0, attn, attn + NEG_INF)
        attn = jax.nn.softmax(attn, axis=-1)
        out = jnp.einsum('bnm,bmo->bno', attn, hidden) + bias
        return out

    h = jnp.maximum(_layernorm(x, axis=-1), 0.0)
    x = x + _L0_gnn_ref(adj, h, L0_gnn_W, L0_gnn_b)
    h = jnp.maximum(_layernorm(x, axis=-1), 0.0)
    x = x + _L1_gnn_ref(h, adj, L1_gnn_W, L1_gnn_a, L1_gnn_bias)
    return x


_drawn_inputs = setup_inputs


def setup_inputs(seed=0):
    import zlib

    import numpy as np

    out = dict(_drawn_inputs(seed))
    spreads = {'L0_gnn_b': (0.0, 0.1)}
    factors = {'L1_gnn_a': 2.941}
    for name, (base, spread) in spreads.items():
        noise = np.random.default_rng([zlib.crc32(name.encode()), seed]).standard_normal(out[name].shape)
        drawn = base * np.exp(spread * noise) if base else spread * noise
        out[name] = jnp.asarray(drawn.astype(out[name].dtype))
    for name, factor in factors.items():
        out[name] = (out[name] * factor).astype(out[name].dtype)
    return out
```

```python
from contextlib import ExitStack

import numpy as np

import concourse.bass as bass
from concourse import mybir

ALU = mybir.AluOpType
ACT = mybir.ActivationFunctionType
AX = mybir.AxisListType
BF16 = mybir.dt.bfloat16
F32 = mybir.dt.float32
I32 = mybir.dt.int32

P = 128
B, N, C = 8, 2048, 256
S = 25
T = 4
QR = T * P
ROWS = B * N
QUADS = ROWS // QR
QB = N // QR
NJ = N // P
LAG = QB
AHEAD = QB + 1
TRING = 2 * QB
RING = 2 * QB
GB = 8
NG = N // GB
TOP = 32
HW = C + 4
KC = C // P
EPS = 1e-5
SLOPE = 0.2
BIG = float(2 ** 40)
RISE = 1.0 - SLOPE
FAR = float(2 ** 60)
LONE = BIG - float(np.float32(RISE)) * FAR
PADKEY = -1000.0
ZERO_ROW = TRING * QR

C_ID, C_BASE, C_J, C_POW, C_PK, C_CODE = 0, P, P + NG, P + NG + GB, P + NG + 2 * GB, P + NG + 2 * GB + P // GB
C_ALL = C_CODE + 2 * QUADS

STEPS = {"index": (-1, QUADS - 2), "gather": (0, QUADS - 1), "project": (0, QUADS - 1),
         "attend": (LAG, QUADS - 1 + LAG)}


def shape_constants():
    c = np.zeros((P, C_ALL), np.float32)
    c[:, C_ID:C_ID + P] = np.eye(P)
    c[:, C_BASE:C_BASE + NG] = (NG - np.arange(NG)) * 2.0 ** GB + (2.0 ** GB - 1)
    c[:, C_J:C_J + GB] = np.arange(GB)
    c[:, C_POW:C_POW + GB] = 2.0 ** np.arange(GB)
    for m in range(P):
        c[m, C_PK + m // GB] = -(2.0 ** (m % GB)) / BIG
    for q in range(QUADS):
        base = N * (q // QB % (TRING // QB) + 1)
        c[:, C_CODE + 2 * q] = base
        c[:, C_CODE + 2 * q + 1] = ZERO_ROW - base
    return c


class Uses:

    def __init__(self, **per_step):
        self.per_step = per_step
        self.n = 0

    def start(self, s, lo):
        self.n = 0
        for kind, uses in self.per_step.items():
            first, last = STEPS[kind]
            if lo > last:
                self.n = self.n + uses * (last - first + 1)
            elif lo >= first:
                self.n = self.n + (s - first) * uses

    def next(self):
        self.n = self.n + 1
        return self.n


class Count:

    def __init__(self):
        self.k = 0

    def next(self):
        self.k += 1
        return self.k


def bank1_uses():
    return Uses(attend=2, gather=T, index=4 * T // 2, project=2 * KC + 3)


def bank2_uses():
    return Uses(gather=T, index=2)


def two_layers(nc, x, adj, w0, b0, w1, a1, bias1, consts, out, table, xmid, nmask):
    rows = lambda ap: ap.rearrange("b n c -> (b n) c")
    x_r, adj_r, out_r = rows(x), rows(adj), rows(out)
    quad = lambda ap, q: ap[bass.ds(q * QR, QR), :].rearrange("(t p) c -> p t c", p=P)
    tile = lambda ap, q, t: ap[bass.ds(q * QR + t * P, P), :]

    with ExitStack() as ctx:
        def sb(name, shape, dt):
            return ctx.enter_context(nc.sbuf_tensor(name, shape, dt))

        def psum(name, shape, dt):
            return ctx.enter_context(nc.psum_tensor(name, shape, dt))

        def sem(name):
            return ctx.enter_context(nc.semaphore(name))

        cst = sb("cst", [P, C_ALL], F32)
        ident_b = sb("ident_b", [P, P], BF16)
        neg_ident = sb("neg_ident", [P, P], BF16)
        pack_w = sb("pack_w", [P, P // GB], BF16)
        pow_i = sb("pow_i", [P, GB], I32)
        ones_f = sb("ones_f", [P, P], F32)
        ones_b = sb("ones_b", [3, P], BF16)
        w0_sb = sb("w0_sb", [P, 2 * KC, C], F32)
        b0_row = sb("b0_row", [1, C], F32)
        bias_b = sb("bias_b", [P, C], F32)
        w1_t = sb("w1_t", [P, KC, C + 2], F32)
        wa2_b = sb("wa2_b", [P, KC, P], F32)
        a_t = sb("a_t", [P, KC, 2], F32)
        ident = cst[:, C_ID:C_ID + P]
        word_base = cst[:, C_BASE:C_BASE + NG]

        near = sb("near", [P, 2, S, C], F32)
        hid = sb("hid", [P, RING * T, HW], F32)
        a2_all = sb("a2_all", [P, RING * QR], F32)
        a1_b = sb("a1_b", [P, QR], F32)
        nm_q = sb("nm_q", [P, T, N], BF16)
        adj_i = sb("adj_i", [P, 2, N], I32)
        nm_t = sb("nm_t", [P, 2, N], BF16)
        nm_x = sb("nm_x", [P, 2, N // 2], BF16)
        lin = sb("lin", [P, 2, QR], F32)
        wgt = sb("wgt", [P, 2, 2 * QR], F32)
        x_ln = sb("x_ln", [P, T, C], F32)
        h_ln = sb("h_ln", [P, T, C], F32)
        h_q = sb("h_q", [P, T, C], F32)
        x_q = sb("x_q", [P, T, C], F32)
        x1_q = sb("x1_q", [P, T, C], F32)
        h2_t = sb("h2_t", [P, KC, QR], F32)
        o_q = sb("o_q", [P, T, C], F32)
        agg = sb("agg", [P, C], F32)
        key = sb("key", [P, 2, NG], F32)
        key2 = sb("key2", [P, 2, NG], F32)
        bits = sb("bits", [P, 2 * NG], I32)
        top = sb("top", [P, 2, TOP], F32)
        top_i = sb("top_i", [P, 2 * TOP], I32)
        high_i = sb("high_i", [P, 2 * TOP], I32)
        code = sb("code", [P, 2], F32)
        big_c = sb("big_c", [P, 1], F32)
        miss = sb("miss", [P, 2, TOP], F32)
        idx = sb("idx", [P, T, TOP], I32)
        stat = sb("stat", [P, 2 * T, 6], F32)
        mv = sb("mv", [P, 2 * T, 2], F32)
        var = sb("var", [P, 2 * T], F32)
        rsq_i = sb("rsq_i", [P, 2 * T], I32)
        rstd = sb("rstd", [P, 2 * T], F32)
        nwt = sb("nwt", [P, 2 * T], F32)
        shift = sb("shift", [P, 2 * T], F32)
        a2_rise = sb("a2_rise", [P, NJ], F32)
        a2_slope = sb("a2_slope", [P, NJ], F32)
        a1_c = sb("a1_c", [P, T], F32)
        amax = sb("amax", [P, T], F32)
        lone = sb("lone", [P, T], F32)
        cmax = sb("cmax", [P, T], F32)
        a1_p = sb("a1_p", [P, T], F32)
        rmax = sb("rmax", [P, T], F32)
        nmax = sb("nmax", [P, T], F32)
        rest = sb("rest", [P, T], F32)
        m_c = sb("m_c", [P, T, 3], BF16)
        m_r = sb("m_r", [3, QR], BF16)
        rden = sb("rden", [P, T], F32)
        acc = psum("acc", [P, T, 512], F32)
        pen = psum("pen", [P, 2, 512], F32)
        bank1 = psum("bank1", [P, 512], F32)
        bank2 = psum("bank2", [P, 512], F32)
        bank1_b = bank1[:, :].bitcast(BF16)

        wgt_flat = wgt[:, :, :].rearrange("p a b -> p (a b)")
        h2_q = wgt_flat[:, 0:T * C].rearrange("p (t c) -> p t c", t=T)
        a2_row = wgt_flat[:, 0:N]
        junk = acc[:, :, :].rearrange("p t c -> p (t c)")
        diag = lin[:, 0, :].rearrange("p (t c) -> p t c", t=T)
        w1_n = wgt_flat[:, 0:KC * C].rearrange("p (k c) -> p k c", k=KC)
        bias_row = wgt_flat[0:1, KC * C:KC * C + C]
        a_rows = wgt_flat[0:2, KC * C + C:KC * C + 2 * C]
        cat_t = h2_t[:, 0, :]
        zeros = agg[0:1, :]

        cst_in, w_in = sem("cst_in"), sem("w_in")
        xln_in, h_in, x_in, x1_in = sem("xln_in"), sem("h_in"), sem("x_in"), sem("x1_in")
        adj_in = [sem("adj_in0"), sem("adj_in1")]
        nm_in = sem("nm_in")
        near_in = [sem("near_in0"), sem("near_in1")]
        zero_out, table_out, x1_out, out_out = sem("zero_out"), sem("table_out"), sem("x1_out"), sem("out_out")
        fill_out = sem("fill_out")
        nm_out = [sem("nm_out0"), sem("nm_out1")]
        set_done = sem("set_done")
        set_act = sem("set_act")
        set_pe = sem("set_pe")
        b1_full, b1_free = sem("b1_full"), sem("b1_free")
        b2_full, b2_free = sem("b2_full"), sem("b2_free")
        ix_step = sem("ix_step")
        idx_ready = sem("idx_ready")
        nm_made = sem("nm_made")
        packed = sem("packed")
        agg_made = sem("agg_made")
        x1_made = sem("x1_made")
        ln_step = sem("ln_step")
        ln1_ready, ln2_ready = sem("ln1_ready"), sem("ln2_ready")
        h_made = sem("h_made")
        h2_made = sem("h2_made")
        hid_made = sem("hid_made")
        a2_made = sem("a2_made")
        as_step = sem("as_step")
        diag_made, m_made = sem("diag_made"), sem("m_made")
        as_act = sem("as_act")
        pen_made = sem("pen_made")
        lin_made = sem("lin_made")
        arg_made = sem("arg_made")
        wgt_made = sem("wgt_made")
        wgt_used = sem("wgt_used")
        af_step = sem("af_step")
        out_made = sem("out_made")

        block = ctx.enter_context(nc.Block())

        def schedule(engine, step):
            step(0, 0, {"gather", "index", "table", "project"})
            with engine.Fori(1, LAG) as s:
                step(s, 1, {"gather", "index", "table", "project"})
            with engine.Fori(LAG, QUADS - AHEAD) as s:
                step(s, LAG, {"gather", "index", "table", "project", "attend", "more"})
            with engine.Fori(QUADS - AHEAD, QUADS - 1) as s:
                step(s, QUADS - AHEAD, {"gather", "index", "project", "attend", "more"})
            step(QUADS - 1, QUADS - 1, {"gather", "project", "attend", "more"})
            with engine.Fori(QUADS, QUADS + LAG - 1) as s:
                step(s, QUADS, {"attend", "more"})
            step(QUADS + LAG - 1, QUADS + LAG - 1, {"attend"})

        @block.sync
        def _(sp):
            sp.dma_start(cst[:, :], consts).then_inc(cst_in, 16)
            sp.dma_start(x_ln[:, :, :], quad(x_r, 0)).then_inc(xln_in, 16)
            sp.dma_start(adj_i[:, 0, :], tile(adj_r, 0, 0)).then_inc(adj_in[0], 16)
            sp.dma_start(adj_i[:, 1, :], tile(adj_r, 0, 1)).then_inc(adj_in[1], 16)
            sp.dma_start(w0_sb[:, :, :], w0.rearrange("(k p) o -> p k o", p=P)).then_inc(w_in, 16)
            sp.dma_start(w1_n, w1.rearrange("(k p) i -> p k i", p=P)).then_inc(w_in, 16)
            sp.dma_start(a_rows, a1).then_inc(w_in, 16)
            sp.dma_start(b0_row[:, :], b0.rearrange("(a d) -> a d", a=1)).then_inc(w_in, 16)
            sp.dma_start(bias_row, bias1.rearrange("(a d) -> a d", a=1)).then_inc(w_in, 16)
            sp.wait_ge(set_done, 1)
            sp.dma_start(table[ZERO_ROW:ZERO_ROW + 1, :], zeros).then_inc(zero_out, 16)

            def store_table(q):
                sp.wait_ge(h_made, T * q + T)
                sp.nop(nofuse=True)
                sp.dma_start(quad(table, q % TRING), h_ln[:, :, :]).then_inc(table_out, 16)

            def load_x_ln(q):
                sp.wait_ge(table_out, 16 * q)
                sp.nop(nofuse=True)
                sp.dma_start(x_ln[:, :, :], quad(x_r, q)).then_inc(xln_in, 16)

            def load_adj(q, t):
                if not (isinstance(q, int) and q == 0 and t < 2):
                    sp.wait_ge(nm_made, T * q + t - 1)
                    sp.nop(nofuse=True)
                sp.dma_start(adj_i[:, t % 2, :], tile(adj_r, q, t)).then_inc(adj_in[t % 2], 16)

            load_adj(0, 2)
            load_adj(0, 3)
            store_table(0)
            for q in range(AHEAD, TRING):
                sp.dma_start(quad(table, q), h_ln[:, :, :]).then_inc(fill_out, 16)
            sp.wait_ge(fill_out, 16 * (TRING - AHEAD))
            with sp.Fori(1, AHEAD) as q:
                load_x_ln(q)
                store_table(q)
            sp.wait_ge(nm_out[0], 32)
            sp.wait_ge(nm_out[1], 32)
            sp.dma_start(nm_q[:, :, :], quad(nmask, 0)).then_inc(nm_in, 16)

            def step(s, lo, stages):
                a = s - LAG
                if "gather" in stages:
                    if lo > 0:
                        sp.wait_ge(x1_made, T * s)
                        sp.nop(nofuse=True)
                    sp.dma_start(h_q[:, :, :], quad(table, s % TRING)).then_inc(h_in, 16)
                    sp.dma_start(x_q[:, :, :], quad(x_r, s)).then_inc(x_in, 16)
                if "attend" in stages:
                    sp.dma_start(o_q[:, :, :], quad(xmid, a)).then_inc(x1_in, 16)
                if "table" in stages:
                    load_x_ln(s + AHEAD)
                if "index" in stages:
                    for t in range(T):
                        load_adj(s + 1, t)
                if "more" in stages:
                    sp.wait_ge(pen_made, NJ * (a + 1))
                    sp.nop(nofuse=True)
                    for u in range(2):
                        sp.wait_ge(nm_out[u], 16 * 2 * (a + 2))
                        sp.nop(nofuse=True)
                    sp.dma_start(nm_q[:, :, :], quad(nmask, a + 1)).then_inc(nm_in, 16)
                if "attend" in stages:
                    sp.wait_ge(out_made, a + 2)
                    sp.nop(nofuse=True)
                    sp.dma_start(quad(out_r, a), o_q[:, :, :]).then_inc(out_out, 16)
                if "gather" in stages:
                    sp.wait_ge(x1_made, T * s + T)
                    sp.nop(nofuse=True)
                    sp.dma_start(quad(xmid, s), x1_q[:, :, :]).then_inc(x1_out, 16)
                if "table" in stages:
                    store_table(s + AHEAD)
                if "attend" in stages:
                    sp.wait_ge(out_out, 16 * (a + 1))
                    sp.nop(nofuse=True)
                if "gather" in stages:
                    sp.wait_ge(x1_out, 16 * (s + 1))
                    sp.nop(nofuse=True)

            schedule(sp, step)
            sp.wait_ge(zero_out, 16)
            sp.wait_ge(table_out, 16 * QUADS)
            sp.wait_ge(nm_out[0], 16 * 2 * QUADS)
            sp.wait_ge(nm_out[1], 16 * 2 * QUADS)
            sp.wait_ge(x1_out, 16 * QUADS)
            sp.wait_ge(out_out, 16 * QUADS)

        @block.gpsimd
        def _(pool):
            pool.wait_ge(zero_out, 16)
            pool.wait_ge(fill_out, 16 * (TRING - AHEAD))

            def step(s, lo, stages):
                if "gather" not in stages:
                    return
                pool.wait_ge(table_out, 16 * (s + QB) if "table" in stages else 16 * QUADS)
                for t in range(T):
                    if t % 2 == 0:
                        pool.wait_ge(idx_ready, 2 * s + t // 2 + 1)
                    pool.wait_ge(agg_made, T * s + t + 1)
                    pool.nop(nofuse=True)
                    for k in range(S):
                        pool.indirect_dma_start(
                            out=near[:, t % 2, k, :], out_offset=None, in_=table,
                            in_offset=bass.IndirectOffsetOnAxis(ap=idx[:, t, k:k + 1], axis=0),
                        ).then_inc(near_in[t % 2], 16)

            schedule(pool, step)

        @block.scalar
        def _(act):
            b1 = bank1_uses()
            act.wait_ge(cst_in, 16)
            nc.scalar.activation(ident_b[:, :], ident, ACT.Copy)
            nc.scalar.activation(neg_ident[:, :], ident, ACT.Copy, scale=-1.0)
            nc.scalar.activation(pack_w[:, :], cst[:, C_PK:C_PK + P // GB], ACT.Copy).then_inc(set_act, 1)

            def setup_weights():
                act.wait_ge(set_pe, 1)
                nc.scalar.activation(w1_t[:, :, 0:C], bank1[:, :].rearrange("p (k c) -> p k c", k=KC),
                                     ACT.Copy).then_inc(set_act, 1)
                act.wait_ge(set_pe, 2)
                nc.scalar.activation(a_t[:, :, :], bank1[:, 0:2 * KC].rearrange("p (k c) -> p k c", k=KC),
                                     ACT.Copy).then_inc(set_act, 1)
                act.wait_ge(set_pe, 3)
                nc.scalar.activation(w1_t[:, :, C:C + 2], bank1[:, 0:2 * KC].rearrange("p (k c) -> p k c", k=KC),
                                     ACT.Copy).then_inc(set_act, 1)
                act.wait_ge(set_pe, 4)
                nc.scalar.activation(bias_b[:, :], bank1[:, 0:C], ACT.Copy)
                act.wait_ge(set_act, 4)
                act.wait_ge(set_done, 2)
                for k in range(KC):
                    ins = nc.scalar.activation(wa2_b[:, k, :], ones_f[:, :], ACT.Copy,
                                               scale=w1_t[:, k, C + 1:C + 2])
                ins.then_inc(set_act, 1)
                act.sem_inc(b1_free, 1)

            def index_prep(q, pair, first):
                for u in range(2):
                    t = 2 * pair + u
                    act.wait_ge(adj_in[u], 16 * (2 * q + pair + 1))
                    if not (first and pair == 0):
                        act.wait_ge(nm_out[u], 16 * (2 * q + pair))
                    nc.scalar.activation(nm_t[:, u, :], adj_i[:, u, :], ACT.Relu, bias=BIG_B, scale=-BIG
                                         ).then_inc(nm_made, 1)
                for u in range(2):
                    t = 2 * pair + u
                    act.wait_ge(nm_made, T * q + t + 1)
                    act.dma_start(tile(nmask, q, t), nm_t[:, u, :]).then_inc(nm_out[u], 16)
                for u in range(2):
                    for half in range(2):
                        h = 4 * pair + 2 * u + half
                        act.wait_ge(b1_full, b1.next())
                        if not (first and h < 2):
                            act.wait_ge(packed, 2 * T * q + h - 1)
                        nc.scalar.activation(nm_x[:, half, :], bank1_b[:, :], ACT.Copy).then_inc(b1_free, 1)

            def normalise(q, first_col, src, dst, ready, made):
                act.wait_ge(ready, q + 1)
                for t in range(T):
                    c = first_col + t
                    nc.scalar.activation(dst[:, t, :], src[:, t, :], ACT.Relu, bias=shift[:, c:c + 1],
                                         scale=rstd[:, c:c + 1]).then_inc(made, 1)

            def project(q):
                for k in range(KC):
                    act.wait_ge(b1_full, b1.next())
                    nc.scalar.activation(h2_t[:, k, :], bank1[:, :], ACT.Copy).then_inc(b1_free, 1)
                for t in range(T):
                    act.wait_ge(b1_full, b1.next())
                    nc.scalar.activation(hid[:, bass.ds((q % RING) * T + t, 1), 1:C + 3], bank1[:, 0:C + 2],
                                         ACT.Copy).then_inc(b1_free, 1)
                act.wait_ge(b1_full, b1.next())
                nc.scalar.activation(a2_all[:, bass.ds((q % RING) * QR, QR)], bank1[:, :], ACT.Copy
                                     ).then_inc(b1_free, 1)
                act.wait_ge(b1_free, b1.n + 1)
                act.sem_inc(hid_made, 1)

            def leaky(a, c):
                for j in (2 * c, 2 * c + 1):
                    act.wait_ge(arg_made, NJ * a + j + 1)
                    nc.scalar.activation(lin[:, j % 2, :], a1_b[:, :], ACT.Relu, bias=a2_rise[:, j:j + 1],
                                         scale=RISE).then_inc(lin_made, 1)

            def chunk(a, c):
                if c + 1 < NJ // 2:
                    leaky(a, c + 1)
                act.wait_ge(arg_made, NJ * a + 2 * c + 4)
                nc.scalar.activation(wgt[:, c % 2, :], wgt[:, c % 2, :], ACT.Exp).then_inc(wgt_made, 1)

            def cat_copy():
                act.wait_ge(b1_full, b1.next())
                nc.scalar.activation(cat_t, bank1[:, :], ACT.Copy).then_inc(b1_free, 1)

            def step(s, lo, stages):
                b1.start(s, lo)
                a = s - LAG
                if "attend" in stages:
                    act.wait_ge(hid_made, a + LAG if lo < QUADS else QUADS)
                    act.wait_ge(out_made, a + 1)
                    nc.scalar.activation(a2_row, a2_all[:, bass.ds((a % RING) // QB * N, N)], ACT.Copy
                                         ).then_inc(a2_made, 1)
                    act.wait_ge(b1_full, b1.next())
                    nc.scalar.activation(a1_b[:, :], bank1[:, :], ACT.Copy).then_inc(b1_free, 1)
                    act.wait_ge(b1_full, b1.next())
                    nc.scalar.activation(m_r[:, :], bank1_b[0:3, 0:QR], ACT.Copy).then_inc(b1_free, 1)
                    act.wait_ge(b1_free, b1.n + 1)
                    leaky(a, 0)
                for t in range(T):
                    if "attend" in stages:
                        chunk(a, 2 * t)
                        chunk(a, 2 * t + 1)
                    if "index" in stages and t == 1:
                        index_prep(s + 1, 0, False)
                    if "gather" in stages:
                        cat_copy()
                if "index" in stages:
                    index_prep(s + 1, 1, False)
                if "project" in stages:
                    if "table" in stages:
                        normalise(s + AHEAD, 0, x_ln, h_ln, ln1_ready, h_made)
                    normalise(s, T, x1_q, h2_q, ln2_ready, h2_made)
                    project(s)

            act.wait_ge(set_done, 3)
            BIG_B = big_c[:, :]
            setup_weights()
            b1.start(-1, -1)
            index_prep(0, 0, True)
            normalise(0, 0, x_ln, h_ln, ln1_ready, h_made)
            with act.Fori(1, AHEAD) as q:
                normalise(q, 0, x_ln, h_ln, ln1_ready, h_made)
            index_prep(0, 1, True)
            schedule(act, step)

        @block.vector
        def _(dve):
            b2 = bank2_uses()

            nc.vector.memset(agg[:, :], 0.0).then_inc(set_done, 1)
            nc.vector.memset(ones_f[:, :], 1.0).then_inc(set_done, 1)
            nc.vector.memset(big_c[:, :], BIG).then_inc(set_done, 1)
            nc.vector.memset(ones_b[:, :], 1.0)
            nc.vector.memset(hid[:, :, 0:1], 1.0)
            dve.wait_ge(cst_in, 16)
            nc.vector.tensor_copy(pow_i[:, :], cst[:, C_POW:C_POW + GB]).then_inc(set_done, 1)
            dve.wait_ge(set_done, 4)
            dve.sem_inc(agg_made, 2)
            dve.sem_inc(b2_free, 1)
            dve.sem_inc(arg_made, 2)
            dve.sem_inc(out_made, 1)
            dve.wait_ge(zero_out, 16)

            def statistics(cols, sources, ready):
                lo, hi = cols
                chain, cnt = ln_step, Count()
                for c, src in sources:
                    ins = nc.vector.bn_stats(stat[:, c, :], src)
                ins.then_inc(chain, 1)
                dve.wait_ge(chain, cnt.next())
                for c, _ in sources:
                    ins = nc.vector.bn_aggr(mv[:, c, :], stat[:, c, :])
                ins.then_inc(chain, 1)
                dve.wait_ge(chain, cnt.next())
                v, y, n = var[:, lo:hi], rstd[:, lo:hi], nwt[:, lo:hi]
                nc.vector.tensor_scalar(v, mv[:, lo:hi, 1], EPS, None, ALU.add).then_inc(chain, 1)
                dve.wait_ge(chain, cnt.next())
                nc.vector.tensor_scalar(rsq_i[:, lo:hi], v.bitcast(I32), 1, None, ALU.arith_shift_right
                                        ).then_inc(chain, 1)
                dve.wait_ge(chain, cnt.next())
                nc.vector.tensor_scalar(y.bitcast(I32), rsq_i[:, lo:hi], -1.0, float(0x5F3759DF), ALU.mult, ALU.add
                                        ).then_inc(chain, 1)
                dve.wait_ge(chain, cnt.next())
                for _ in range(3):
                    nc.vector.tensor_tensor(n, y, y, ALU.mult).then_inc(chain, 1)
                    dve.wait_ge(chain, cnt.next())
                    nc.vector.scalar_tensor_tensor(n, n, -0.5, v, ALU.mult, ALU.mult).then_inc(chain, 1)
                    dve.wait_ge(chain, cnt.next())
                    nc.vector.scalar_tensor_tensor(y, n, 1.5, y, ALU.add, ALU.mult).then_inc(chain, 1)
                    dve.wait_ge(chain, cnt.next())
                nc.vector.scalar_tensor_tensor(shift[:, lo:hi], mv[:, lo:hi, 0], -1.0, y, ALU.mult, ALU.mult
                                               ).then_inc(ready, 1)
                dve.sem_clear(chain)

            def table_alone(q):
                dve.wait_ge(xln_in, 16 * (q + 1))
                statistics((0, T), [(t, x_ln[:, t, :]) for t in range(T)], ln1_ready)

            def statistics_of_step(s, stages):
                dve.wait_ge(x1_made, T * s + T)
                if "table" in stages:
                    dve.wait_ge(xln_in, 16 * (s + AHEAD + 1))
                    cols, src = (0, 2 * T), [(t, x_ln[:, t, :]) for t in range(T)]
                else:
                    cols, src = (T, 2 * T), []
                src = src + [(T + t, x1_q[:, t, :]) for t in range(T)]
                statistics(cols, src, ln2_ready)
                if "table" in stages:
                    dve.wait_ge(ln2_ready, s + 1)
                    dve.sem_inc(ln1_ready, 1)

            def top_rounds(src, ix_n):
                for r in range(TOP // 8):
                    seen = []
                    for u in range(2):
                        if r > 0:
                            dve.wait_ge(ix_step, gone[u])
                        nc.vector.max(top[:, u, 8 * r:8 * r + 8], src[:, u, :]).then_inc(ix_step, 1)
                        seen.append(ix_n.next())
                    gone = []
                    if r < TOP // 8 - 1:
                        for u in range(2):
                            dve.wait_ge(ix_step, seen[u])
                            nc.vector.match_replace(src[:, u, :], top[:, u, 8 * r:8 * r + 8], src[:, u, :], PADKEY
                                                    ).then_inc(ix_step, 1)
                            gone.append(ix_n.next())
                dve.wait_ge(ix_step, seen[1])

            def index(q, pair):
                ix_n = Count()
                words = bank2[:, :].rearrange("p (u g) -> p u g", u=2)
                dve.wait_ge(b2_full, b2.next())
                base = word_base.unsqueeze(1).to_broadcast([P, 2, NG])
                nc.vector.scalar_tensor_tensor(key2[:, :, :], words, -(2.0 ** GB - 1.5), base, ALU.is_gt, ALU.mult
                                               ).then_inc(ix_step, 1)
                dve.wait_ge(ix_step, ix_n.next())
                nc.vector.tensor_tensor(key[:, :, :], key2[:, :, :], words, ALU.add).then_inc(b2_free, 1)
                nc.vector.tensor_copy(code[:, :], cst[:, bass.ds(q * 2 + C_CODE, 2)]).then_inc(ix_step, 1)
                dve.wait_ge(ix_step, ix_n.next())
                top_rounds(key, ix_n)
                nc.vector.tensor_scalar(top_i[:, :], top[:, :, :].rearrange("p u k -> p (u k)"), 0.0, None, ALU.max
                                        ).then_inc(ix_step, 1)
                dve.wait_ge(ix_step, ix_n.next())
                words_i = top_i[:, :].unsqueeze(2).to_broadcast([P, 2 * TOP, GB])
                powers = pow_i[:, :].unsqueeze(1).to_broadcast([P, 2 * TOP, GB])
                nc.vector.tensor_tensor(bits[:, :].rearrange("p (k j) -> p k j", j=GB), words_i, powers,
                                        ALU.bitwise_and).then_inc(ix_step, 1)
                ix_n.next()
                nc.vector.tensor_scalar(high_i[:, :], top_i[:, :], (2 ** GB - 1) ^ 0xFFFFF, None, ALU.bitwise_and
                                        ).then_inc(ix_step, 1)
                dve.wait_ge(ix_step, ix_n.next())
                high = high_i[:, :].unsqueeze(2).to_broadcast([P, 2 * TOP, GB])
                place = cst[:, C_J:C_J + GB].unsqueeze(1).to_broadcast([P, 2 * TOP, GB])
                nc.vector.scalar_tensor_tensor(
                    key2[:, :, :].rearrange("p u (k j) -> p (u k) j", j=GB), high, GB / 2.0 ** GB, place,
                    ALU.mult, ALU.subtract).then_inc(ix_step, 1)
                dve.wait_ge(ix_step, ix_n.next())
                nc.vector.scalar_tensor_tensor(
                    key[:, :, :].rearrange("p u g -> p (u g)"), bits[:, :], 0.0,
                    key2[:, :, :].rearrange("p u g -> p (u g)"), ALU.is_gt, ALU.mult).then_inc(ix_step, 1)
                dve.wait_ge(ix_step, ix_n.next())
                top_rounds(key, ix_n)
                nc.vector.tensor_scalar(miss[:, :, :], top[:, :, :], 0.0, code[:, 1:2], ALU.is_equal, ALU.mult
                                        ).then_inc(ix_step, 1)
                dve.wait_ge(ix_step, ix_n.next())
                nc.vector.scalar_tensor_tensor(idx[:, 2 * pair:2 * pair + 2, :], miss[:, :, :], code[:, 0:1],
                                               top[:, :, :], ALU.add, ALU.subtract).then_inc(idx_ready, 1)
                dve.sem_clear(ix_step)

            def maximum(s, t):
                dve.wait_ge(near_in[t % 2], 16 * S * (2 * s + t // 2 + 1))
                nc.vector.tensor_reduce(agg[:, :], near[:, t % 2, :, :].rearrange("p k c -> p c k"), AX.X, ALU.max
                                        ).then_inc(agg_made, 1)

            def residual0(s, t, lo):
                if t == 0:
                    dve.wait_ge(x_in, 16 * (s + 1))
                    dve.wait_ge(h_in, 16 * (s + 1))
                    if lo > 0:
                        dve.wait_ge(h2_made, T * s)
                dve.wait_ge(b2_full, b2.next())
                nc.vector.scalar_tensor_tensor(x1_q[:, t, :], bank2[:, 0:C], 0.0, x_q[:, t, :], ALU.max, ALU.add
                                               ).then_inc(b2_free, 1)
                dve.wait_ge(b2_free, b2.n + 1)
                dve.sem_inc(x1_made, 1)

            def attend_setup(a):
                as_n = Count()
                dve.wait_ge(nm_in, 16 * (a + 1))
                dve.wait_ge(a2_made, a + 1)
                batch = (a % RING) // QB
                nc.vector.tensor_scalar(a2_rise[:, :], hid[:, bass.ds(batch * NJ, NJ), C + 2], RISE, None, ALU.mult)
                nc.vector.tensor_scalar(a2_slope[:, :], hid[:, bass.ds(batch * NJ, NJ), C + 2], SLOPE, None, ALU.mult)
                nc.vector.tensor_copy(a1_c[:, :], hid[:, bass.ds((a % RING) * T, T), C + 1]).then_inc(as_step, 1)
                as_n.next()
                for t in range(T):
                    nc.vector.tensor_tensor_reduce(
                        out=junk, in0=a2_row, in1=nm_q[:, t, :], scale=1.0,
                        scalar=-3.0e38, op0=ALU.subtract, op1=ALU.max, accum_out=amax[:, t:t + 1]
                        ).then_inc(as_step, 1)
                    dve.wait_ge(as_step, as_n.next())
                nc.vector.tensor_scalar(lone[:, :], amax[:, :], -BIG / 2, None, ALU.is_lt).then_inc(as_step, 1)
                lone_n = as_n.next()
                nc.vector.scalar_tensor_tensor(cmax[:, :], amax[:, :], -BIG / 2, amax[:, :], ALU.is_ge, ALU.mult
                                               ).then_inc(as_step, 1)
                as_n.next()
                dve.wait_ge(as_step, lone_n)
                nc.vector.scalar_tensor_tensor(a1_p[:, :], lone[:, :], FAR, a1_c[:, :], ALU.mult, ALU.add
                                               ).then_inc(as_step, 1)
                dve.wait_ge(as_step, as_n.next())
                nc.vector.tensor_tensor(diag, ident.unsqueeze(1).to_broadcast([P, T, P]),
                                        a1_p[:, :].unsqueeze(2).to_broadcast([P, T, P]), ALU.mult
                                        ).then_inc(diag_made, 1)
                nc.vector.tensor_tensor(rest[:, :], a1_c[:, :], cmax[:, :], ALU.add).then_inc(as_step, 1)
                dve.wait_ge(as_step, as_n.next())
                nc.vector.scalar_tensor_tensor(rmax[:, :], rest[:, :], SLOPE, rest[:, :], ALU.mult, ALU.max
                                               ).then_inc(as_step, 1)
                dve.wait_ge(as_step, as_n.next())
                nc.vector.scalar_tensor_tensor(rest[:, :], a1_c[:, :], SLOPE, rmax[:, :], ALU.mult, ALU.subtract
                                               ).then_inc(as_step, 1)
                dve.wait_ge(as_step, as_n.next())
                nc.vector.scalar_tensor_tensor(nmax[:, :], lone[:, :], LONE, rest[:, :], ALU.mult, ALU.add
                                               ).then_inc(as_step, 1)
                dve.wait_ge(as_step, as_n.next())
                nc.vector.tensor_copy(m_c[:, :, 0], nmax[:, :]).then_inc(as_step, 1)
                dve.wait_ge(as_step, as_n.next())
                nc.vector.tensor_tensor(rest[:, :], nmax[:, :], m_c[:, :, 0], ALU.subtract).then_inc(as_step, 1)
                dve.wait_ge(as_step, as_n.next())
                nc.vector.tensor_copy(m_c[:, :, 1], rest[:, :]).then_inc(as_step, 1)
                dve.wait_ge(as_step, as_n.next())
                nc.vector.tensor_tensor(m_c[:, :, 2], rest[:, :], m_c[:, :, 1], ALU.subtract).then_inc(m_made, 1)
                dve.sem_clear(as_step)

            def chunk(a, c):
                dve.wait_ge(wgt_used, NJ // 2 * a + c + 1)
                for i in range(2):
                    j = 2 * c + i
                    dve.wait_ge(pen_made, NJ * a + j + 1)
                    dve.wait_ge(lin_made, NJ * a + j + 1)
                    nc.vector.scalar_tensor_tensor(wgt[:, c % 2, i * QR:(i + 1) * QR], pen[:, j % 2, :],
                                                   a2_slope[:, j:j + 1], lin[:, j % 2, :], ALU.add, ALU.add
                                                   ).then_inc(arg_made, 1)

            def attend_end(a):
                af_n = Count()
                dve.wait_ge(wgt_used, NJ // 2 * (a + 1) + 2)
                dve.wait_ge(x1_in, 16 * (a + 1))
                nc.vector.reciprocal(rden[:, :], acc[:, :, 0]).then_inc(af_step, 1)
                dve.wait_ge(af_step, af_n.next())
                for t in range(T):
                    ins = nc.vector.scalar_tensor_tensor(near_out[:, t, :], acc[:, t, 1:C + 1], rden[:, t:t + 1],
                                                         bias_b[:, :], ALU.mult, ALU.add)
                ins.then_inc(af_step, 1)
                dve.wait_ge(af_step, af_n.next())
                nc.vector.tensor_tensor(o_q[:, :, :], near_out[:, :, :], o_q[:, :, :], ALU.add).then_inc(out_made, 1)
                dve.sem_clear(af_step)

            def step(s, lo, stages):
                b2.start(s, lo)
                a = s - LAG
                if "attend" in stages:
                    attend_setup(a)
                for t in range(T):
                    if "attend" in stages:
                        chunk(a, 2 * t)
                        chunk(a, 2 * t + 1)
                    if "gather" in stages:
                        if t % 2 == 1:
                            residual0(s, t - 1, lo)
                        maximum(s, t)
                        if t == 1:
                            if "index" in stages:
                                index(s + 1, 0)
                            residual0(s, t, lo)
                if "attend" in stages:
                    attend_end(a)
                if "gather" in stages:
                    residual0(s, T - 1, lo)
                    statistics_of_step(s, stages)
                if "index" in stages:
                    index(s + 1, 1)

            near_out = wgt_flat[:, 0:T * C].rearrange("p (t c) -> p t c", t=T)
            b2.start(-1, -1)
            table_alone(0)
            with dve.Fori(1, AHEAD) as q:
                table_alone(q)
            index(0, 0)
            index(0, 1)
            schedule(dve, step)

        @block.tensor
        def _(pe):
            b1, b2 = bank1_uses(), bank2_uses()

            def setup_weights():
                pe.wait_ge(w_in, 80)
                pe.wait_ge(cst_in, 16)
                for o in range(KC):
                    for i in range(KC):
                        mm = nc.tensor.transpose(bank1[:, i * C + o * P:i * C + (o + 1) * P],
                                                 w1_n[:, o, i * P:(i + 1) * P], ident)
                mm.then_inc(set_pe, 1)
                pe.wait_ge(set_act, 2)
                for o in range(KC):
                    mm = nc.tensor.transpose(bank1[:, 2 * o:2 * o + 2], a_rows[:, o * P:(o + 1) * P], ident[0:2, 0:2])
                mm.then_inc(set_pe, 1)
                pe.wait_ge(set_act, 3)
                for i in range(KC):
                    for o in range(KC):
                        mm = nc.tensor.matmul(bank1[:, 2 * i:2 * i + 2], w1_n[:, o, i * P:(i + 1) * P], a_t[:, o, :],
                                              start=(o == 0), stop=(o == KC - 1))
                mm.then_inc(set_pe, 1)
                pe.wait_ge(set_act, 4)
                pe.wait_ge(set_done, 2)
                nc.tensor.matmul(bank1[:, 0:C], ones_f[0:1, :], bias_row, start=True, stop=True
                                 ).then_inc(set_pe, 1)
                pe.wait_ge(set_act, 5)
                pe.wait_ge(set_done, 4)
                pe.sem_inc(wgt_used, 2)

            def index_prep(q, pair):
                bank2_free = b2.next()
                for u in range(2):
                    pe.wait_ge(nm_made, T * q + 2 * pair + u + 1)
                    for half in range(2):
                        pe.wait_ge(b1_free, b1.next())
                        for i in range(NJ // 2):
                            j = half * NJ // 2 + i
                            mm = nc.tensor.transpose(bank1_b[:, i * P:(i + 1) * P], nm_t[:, u, j * P:(j + 1) * P],
                                                     ident_b[:, :])
                        mm.then_inc(b1_full, 1)
                        if u == 0 and half == 0:
                            pe.wait_ge(b2_free, bank2_free)
                        pe.wait_ge(b1_free, b1.n + 1)
                        for i in range(NJ // 2):
                            j = half * NJ // 2 + i
                            w = P // GB
                            mm = nc.tensor.matmul(bank2[:, u * NG + j * w:u * NG + (j + 1) * w],
                                                  nm_x[:, half, i * P:(i + 1) * P], pack_w[:, :],
                                                  start=True, stop=True)
                        mm.then_inc(packed, 1)
                pe.wait_ge(packed, 2 * T * q + 4 * pair + 4)
                pe.sem_inc(b2_full, 1)

            def layer0(s, t):
                if t == 0:
                    pe.wait_ge(h_in, 16 * (s + 1))
                pe.wait_ge(agg_made, T * s + t + 3)
                pe.wait_ge(b1_free, b1.next())
                for k in range(KC):
                    nc.tensor.transpose(bank1[:, k * P:(k + 1) * P], h_q[:, t, k * P:(k + 1) * P], ident)
                for k in range(KC):
                    mm = nc.tensor.transpose(bank1[:, (KC + k) * P:(KC + k + 1) * P], agg[:, k * P:(k + 1) * P],
                                             ident)
                mm.then_inc(b1_full, 1)
                pe.wait_ge(b1_free, b1.n + 1)
                pe.wait_ge(b2_free, b2.next())
                for k in range(2 * KC):
                    nc.tensor.matmul(bank2[:, 0:C], cat_t[:, k * P:(k + 1) * P], w0_sb[:, k, :],
                                     start=(k == 0), stop=False)
                nc.tensor.matmul(bank2[:, 0:C], ones_f[0:1, :], b0_row[:, :], start=False, stop=True
                                 ).then_inc(b2_full, 1)

            def project(q):
                pe.wait_ge(h2_made, T * q + T)
                for k in range(KC):
                    pe.wait_ge(b1_free, b1.next())
                    for t in range(T):
                        mm = nc.tensor.transpose(bank1[:, t * P:(t + 1) * P], h2_q[:, t, k * P:(k + 1) * P], ident)
                    mm.then_inc(b1_full, 1)
                for t in range(T):
                    pe.wait_ge(b1_free, b1.next())
                    for k in range(KC):
                        mm = nc.tensor.matmul(bank1[:, 0:C + 2], h2_t[:, k, t * P:(t + 1) * P], w1_t[:, k, :],
                                              start=(k == 0), stop=(k == KC - 1))
                    mm.then_inc(b1_full, 1)
                pe.wait_ge(b1_free, b1.next())
                for k in range(KC):
                    mm = nc.tensor.matmul(bank1[:, :], wa2_b[:, k, :], h2_t[:, k, :], start=(k == 0),
                                          stop=(k == KC - 1))
                mm.then_inc(b1_full, 1)

            def attend_setup(a):
                pe.wait_ge(diag_made, a + 1)
                pe.wait_ge(b1_free, b1.next())
                nc.tensor.matmul(bank1[:, :], ones_f[:, :], lin[:, 0, :], start=True, stop=True).then_inc(b1_full, 1)
                pe.wait_ge(m_made, a + 1)
                pe.wait_ge(b1_free, b1.next())
                for t in range(T):
                    mm = nc.tensor.transpose(bank1_b[0:3, t * P:(t + 1) * P], m_c[:, t, :], ident_b[:, :])
                mm.then_inc(b1_full, 1)
                pe.wait_ge(b1_free, b1.n + 1)
                penalty(a, 0)

            def penalty(a, c):
                for j in (2 * c, 2 * c + 1):
                    pe.wait_ge(arg_made, NJ * a + j + 1)
                    nc.tensor.matmul(pen[:, j % 2, :], ones_b[:, :], m_r[:, :], start=True, stop=False,
                                     skip_group_check=True)
                    for t in range(T):
                        mm = nc.tensor.matmul(pen[:, j % 2, t * P:(t + 1) * P], nm_q[:, t, j * P:(j + 1) * P],
                                              neg_ident[:, :], start=False, stop=(t == T - 1),
                                              skip_group_check=True)
                    mm.then_inc(pen_made, 1)

            def chunk(a, c):
                if c + 1 < NJ // 2:
                    penalty(a, c + 1)
                pe.wait_ge(wgt_made, NJ // 2 * a + c + 1)
                if c == 0:
                    pe.wait_ge(out_made, a + 1)
                batch = (a % RING) // QB
                for i in range(2):
                    j = 2 * c + i
                    for t in range(T):
                        mm = nc.tensor.matmul(
                            acc[:, t, 0:C + 1], wgt[:, c % 2, i * QR + t * P:i * QR + (t + 1) * P],
                            hid[:, bass.ds(batch * NJ + j, 1), 0:C + 1].rearrange("p a c -> p (a c)"),
                            start=(j == 0), stop=(j == NJ - 1), skip_group_check=True)
                mm.then_inc(wgt_used, 1)

            def step(s, lo, stages):
                b1.start(s, lo)
                b2.start(s, lo)
                a = s - LAG
                if "attend" in stages:
                    attend_setup(a)
                for t in range(T):
                    if "attend" in stages:
                        chunk(a, 2 * t)
                        chunk(a, 2 * t + 1)
                    if "gather" in stages:
                        if t == 1 and "index" in stages:
                            index_prep(s + 1, 0)
                        layer0(s, t)
                if "index" in stages:
                    index_prep(s + 1, 1)
                if "project" in stages:
                    project(s)

            setup_weights()
            b1.start(-1, -1)
            b2.start(-1, -1)
            index_prep(0, 0)
            index_prep(0, 1)
            schedule(pe, step)


_INS = ["x", "adj", "L0_gnn_W", "L0_gnn_b", "L1_gnn_W", "L1_gnn_a", "L1_gnn_bias"]


def kernel(**inputs):
    import concourse.bacc as _bacc
    from concourse.bass_utils import run_bass_kernel_spmd as _run

    nc = _bacc.Bacc("TRN2", target_bir_lowering=False, num_devices=1)
    arrays, args = {}, []
    laid_out = [(name, np.ascontiguousarray(inputs[name])) for name in _INS] + [("consts", shape_constants())]
    for name, a in laid_out:
        arrays[f"in_{name}_dram"] = a
        args.append(nc.dram_tensor(f"in_{name}_dram", a.shape, mybir.dt.from_np(a.dtype), kind="ExternalInput").ap())
    out = nc.dram_tensor("out_0_dram", (B, N, C), F32, kind="ExternalOutput").ap()
    table = nc.dram_tensor("table_dram", (ZERO_ROW + 1, C), F32, kind="Internal").ap()
    xmid = nc.dram_tensor("xmid_dram", (ROWS, C), F32, kind="Internal").ap()
    nmask = nc.dram_tensor("nmask_dram", (ROWS, N), BF16, kind="Internal").ap()
    two_layers(nc, *args, out, table, xmid, nmask)
    r = _run(nc, [arrays], core_ids=[0])
    return r.results[0]["out_0_dram"]
```

```python
from contextlib import ExitStack

import numpy as np

import concourse.bass as bass
from concourse import mybir

ALU = mybir.AluOpType
ACT = mybir.ActivationFunctionType
AX = mybir.AxisListType
BF16 = mybir.dt.bfloat16
F32 = mybir.dt.float32
I32 = mybir.dt.int32

P = 128
B, N, C = 8, 2048, 256
S = 25
T = 4
QR = T * P
ROWS = B * N
QUADS = ROWS // QR
QB = N // QR
NJ = N // P
LAG = QB
AHEAD = QB + 1
TRING = 2 * QB
RING = 2 * QB
GB = 8
NG = N // GB
TOP = 32
HW = C + 4
KC = C // P
EPS = 1e-5
SLOPE = 0.2
BIG = float(2 ** 40)
RISE = 1.0 - SLOPE
FAR = float(2 ** 60)
LONE = BIG - float(np.float32(RISE)) * FAR
PADKEY = -1000.0
ZERO_ROW = TRING * QR

C_ID, C_BASE, C_J, C_POW, C_PK, C_CODE = 0, P, P + NG, P + NG + GB, P + NG + 2 * GB, P + NG + 2 * GB + P // GB
C_ALL = C_CODE + 2 * QUADS

STEPS = {
    "index": (-1, QUADS - 2),
    "load_index": (0, QUADS - 3),
    "table": (0, QUADS - 1 - AHEAD),
    "table_rows": (1, QUADS - AHEAD),
    "gather": (0, QUADS - 1),
    "project": (1, QUADS),
    "attend": (LAG, QUADS - 1 + LAG),
    "more": (LAG, QUADS - 2 + LAG),
}


def shape_constants():
    c = np.zeros((P, C_ALL), np.float32)
    c[:, C_ID:C_ID + P] = np.eye(P)
    c[:, C_BASE:C_BASE + NG] = (NG - np.arange(NG)) * 2.0 ** GB + (2.0 ** GB - 1)
    c[:, C_J:C_J + GB] = np.arange(GB)
    c[:, C_POW:C_POW + GB] = 2.0 ** np.arange(GB)
    for m in range(P):
        c[m, C_PK + m // GB] = -(2.0 ** (m % GB)) / BIG
    for q in range(QUADS):
        base = N * (q // QB % (TRING // QB) + 1)
        c[:, C_CODE + 2 * q] = base
        c[:, C_CODE + 2 * q + 1] = ZERO_ROW - base
    return c


class Uses:

    def __init__(self, **per_step):
        self.per_step = per_step
        self.n = 0

    def start(self, s, lo):
        self.n = 0
        for kind, uses in self.per_step.items():
            first, last = STEPS[kind]
            if lo > last:
                self.n = self.n + uses * (last - first + 1)
            elif lo >= first:
                self.n = self.n + (s - first) * uses

    def next(self):
        self.n = self.n + 1
        return self.n


class Count:

    def __init__(self, done=0):
        self.k = done

    def next(self):
        self.k += 1
        return self.k


def bank1_uses():
    return Uses(attend=2, gather=T, index=4 * T // 2, project=1)


def bank2_uses():
    return Uses(gather=T, index=2)


def two_layers(nc, x, adj, w0, b0, w1, a1, bias1, consts, out, table, xmid, nmask):
    rows = lambda ap: ap.rearrange("b n c -> (b n) c")
    x_r, adj_r, out_r = rows(x), rows(adj), rows(out)
    quad = lambda ap, q: ap[bass.ds(q * QR, QR), :].rearrange("(t p) c -> p t c", p=P)
    tile = lambda ap, q, t: ap[bass.ds(q * QR + t * P, P), :]

    with ExitStack() as ctx:
        def sb(name, shape, dt):
            return ctx.enter_context(nc.sbuf_tensor(name, shape, dt))

        def psum(name, shape, dt):
            return ctx.enter_context(nc.psum_tensor(name, shape, dt))

        def sem(name):
            return ctx.enter_context(nc.semaphore(name))

        cst = sb("cst", [P, C_ALL], F32)
        ident_b = sb("ident_b", [P, P], BF16)
        neg_ident = sb("neg_ident", [P, P], BF16)
        pack_w = sb("pack_w", [P, P // GB], BF16)
        pow_i = sb("pow_i", [P, GB], I32)
        ones_f = sb("ones_f", [P, P], F32)
        ones_b = sb("ones_b", [3, P], BF16)
        w0_sb = sb("w0_sb", [P, 2 * KC, C], F32)
        b0_row = sb("b0_row", [1, C], F32)
        bias_b = sb("bias_b", [P, C], F32)
        w1_t = sb("w1_t", [P, KC, C + 2], F32)
        wa2_b = sb("wa2_b", [P, KC, P], F32)
        a_t = sb("a_t", [P, KC, 2], F32)
        ident = cst[:, C_ID:C_ID + P]
        word_base = cst[:, C_BASE:C_BASE + NG]

        near = sb("near", [P, 2, S, C], F32)
        hid = sb("hid", [P, RING * T, HW], F32)
        a2_all = sb("a2_all", [P, RING * QR], F32)
        a1_b = sb("a1_b", [P, QR], F32)
        nm_q = sb("nm_q", [P, T, N], BF16)
        adj_i = sb("adj_i", [P, 2, N], I32)
        nm_t = sb("nm_t", [P, 2, N], BF16)
        nm_x = sb("nm_x", [P, 2, N // 2], BF16)
        lin = sb("lin", [P, 2, QR], F32)
        wgt = sb("wgt", [P, 2, 2 * QR], F32)
        x_ln = sb("x_ln", [P, T, C], F32)
        h_ln = sb("h_ln", [P, T, C], F32)
        h_q = sb("h_q", [P, T, C], F32)
        x_q = sb("x_q", [P, T, C], F32)
        x1_q = sb("x1_q", [P, T, C], F32)
        h2_t = sb("h2_t", [P, KC, QR], F32)
        o_q = sb("o_q", [P, T, C], F32)
        agg = sb("agg", [P, C], F32)
        key = sb("key", [P, 2, NG], F32)
        key2 = sb("key2", [P, 2, NG], F32)
        bits = sb("bits", [P, 2 * NG], I32)
        top = sb("top", [P, 2, TOP], F32)
        top_i = sb("top_i", [P, 2 * TOP], I32)
        high_i = sb("high_i", [P, 2 * TOP], I32)
        code = sb("code", [P, 2], F32)
        big_c = sb("big_c", [P, 1], F32)
        miss = sb("miss", [P, 2, TOP], F32)
        idx = sb("idx", [P, T, TOP], I32)
        stat = sb("stat", [P, NJ, 6], F32)
        mv = sb("mv", [P, NJ, 2], F32)
        var = sb("var", [P, NJ], F32)
        rsq_i = sb("rsq_i", [P, NJ], I32)
        rstd = sb("rstd", [P, NJ], F32)
        nwt = sb("nwt", [P, NJ], F32)
        shift = sb("shift", [P, NJ], F32)
        a2_rise = sb("a2_rise", [P, NJ], F32)
        a2_slope = sb("a2_slope", [P, NJ], F32)
        a1_c = sb("a1_c", [P, T], F32)
        amax = sb("amax", [P, T], F32)
        lone = sb("lone", [P, T], F32)
        cmax = sb("cmax", [P, T], F32)
        a1_p = sb("a1_p", [P, T], F32)
        rmax = sb("rmax", [P, T], F32)
        nmax = sb("nmax", [P, T], F32)
        rest = sb("rest", [P, T], F32)
        m_c = sb("m_c", [P, T, 3], BF16)
        m_r = sb("m_r", [3, QR], BF16)
        rden = sb("rden", [P, T], F32)
        acc = psum("acc", [P, T, 512], F32)
        pen = psum("pen", [P, 2, 512], F32)
        bank1 = psum("bank1", [P, 512], F32)
        bank2 = psum("bank2", [P, 512], F32)
        bank1_b = bank1[:, :].bitcast(BF16)

        wgt_flat = wgt[:, :, :].rearrange("p a b -> p (a b)")
        h2_q = wgt_flat[:, 0:T * C].rearrange("p (t c) -> p t c", t=T)
        a2_row = wgt_flat[:, 0:N]
        junk = lin[:, :, :].rearrange("p a b -> p (a b)").bitcast(BF16)
        x_first = near[:, 0, 0:NJ, :]
        h_first = near[:, 1, 0:NJ, :]
        diag = lin[:, 0, :].rearrange("p (t c) -> p t c", t=T)
        w1_n = wgt_flat[:, 0:KC * C].rearrange("p (k c) -> p k c", k=KC)
        bias_row = wgt_flat[0:1, KC * C:KC * C + C]
        a_rows = wgt_flat[0:2, KC * C + C:KC * C + 2 * C]
        cat_t = h2_t[:, 0, :]
        zeros = agg[0:1, :]

        cst_in, w_in, first_in = sem("cst_in"), sem("w_in"), sem("first_in")
        first_out = sem("first_out")
        xln_in, h_in, x_in, x1_in = sem("xln_in"), sem("h_in"), sem("x_in"), sem("x1_in")
        adj_in = [sem("adj_in0"), sem("adj_in1")]
        nm_in = sem("nm_in")
        near_in = [sem("near_in0"), sem("near_in1")]
        zero_out, table_out, x1_out, out_out = sem("zero_out"), sem("table_out"), sem("x1_out"), sem("out_out")
        fill_out = sem("fill_out")
        nm_out = [sem("nm_out0"), sem("nm_out1")]
        set_done = sem("set_done")
        set_act = sem("set_act")
        set_pe = sem("set_pe")
        b1_full, b1_free = sem("b1_full"), sem("b1_free")
        b2_full, b2_free = sem("b2_full"), sem("b2_free")
        ix_step = sem("ix_step")
        idx_ready = sem("idx_ready")
        nm_made = sem("nm_made")
        nmx_made = sem("nmx_made")
        packed = sem("packed")
        agg_made = sem("agg_made")
        x1_made = sem("x1_made")
        ln_step = sem("ln_step")
        ln1_ready, ln2_ready = sem("ln1_ready"), sem("ln2_ready")
        h_made = sem("h_made")
        first_ready, first_made = sem("first_ready"), sem("first_made")
        h2_made = sem("h2_made")
        proj_pe = sem("proj_pe")
        h2t_made = sem("h2t_made")
        hid_made = sem("hid_made")
        a2_made = sem("a2_made")
        as_step = sem("as_step")
        diag_made, m_made = sem("diag_made"), sem("m_made")
        as_act = sem("as_act")
        pen_made = sem("pen_made")
        lin_made = sem("lin_made")
        arg_made = sem("arg_made")
        wgt_made = sem("wgt_made")
        wgt_used = sem("wgt_used")
        af_step = sem("af_step")
        out_made = sem("out_made")

        block = ctx.enter_context(nc.Block())

        def schedule(engine, step):
            edges = sorted({s for first, last in STEPS.values() for s in (max(first, 0), last + 1)})
            for lo, hi in zip(edges, edges[1:]):
                stages = {kind for kind, (first, last) in STEPS.items() if first <= lo <= last}
                if hi - lo == 1:
                    step(lo, lo, stages)
                else:
                    with engine.Fori(lo, hi) as s:
                        step(s, lo, stages)

        @block.sync
        def _(sp):
            sp.dma_start(cst[:, :], consts).then_inc(cst_in, 16)
            batch0 = lambda ap: ap[0:N, :].rearrange("(t p) c -> p t c", p=P)
            sp.dma_start(x_first, batch0(x_r)).then_inc(first_in, 16)
            sp.dma_start(adj_i[:, 0, :], tile(adj_r, 0, 0)).then_inc(adj_in[0], 16)
            sp.dma_start(adj_i[:, 1, :], tile(adj_r, 0, 1)).then_inc(adj_in[1], 16)
            sp.wait_ge(set_done, 1)
            sp.dma_start(table[ZERO_ROW:ZERO_ROW + 1, :], zeros).then_inc(zero_out, 16)
            sp.dma_start(w1_n, w1.rearrange("(k p) i -> p k i", p=P)).then_inc(w_in, 16)
            sp.dma_start(a_rows, a1).then_inc(w_in, 16)
            sp.dma_start(bias_row, bias1.rearrange("(a d) -> a d", a=1)).then_inc(w_in, 16)
            sp.dma_start(b0_row[:, :], b0.rearrange("(a d) -> a d", a=1)).then_inc(w_in, 16)
            sp.dma_start(w0_sb[:, :, :], w0.rearrange("(k p) o -> p k o", p=P)).then_inc(w_in, 16)
            sp.dma_start(x_ln[:, :, :], quad(x_r, QB)).then_inc(xln_in, 16)

            def store_table(q):
                sp.wait_ge(h_made, T * (q - QB) + T)
                sp.nop(nofuse=True)
                sp.dma_start(quad(table, q % TRING), h_ln[:, :, :]).then_inc(table_out, 16)

            def load_x_ln(q):
                sp.wait_ge(table_out, 16 * (q - QB))
                sp.nop(nofuse=True)
                sp.dma_start(x_ln[:, :, :], quad(x_r, q)).then_inc(xln_in, 16)

            def load_adj(q, t):
                if not (isinstance(q, int) and q == 0 and t < 2):
                    sp.wait_ge(nm_made, T * q + t - 1)
                    sp.nop(nofuse=True)
                sp.dma_start(adj_i[:, t % 2, :], tile(adj_r, q, t)).then_inc(adj_in[t % 2], 16)

            sp.wait_ge(first_made, NJ)
            sp.dma_start(batch0(table), h_first).then_inc(first_out, 16)
            sp.dma_start(table[N:2 * N, :].rearrange("(t p) c -> p t c", p=P), h_first).then_inc(fill_out, 16)
            load_adj(0, 2)
            load_adj(0, 3)
            load_adj(1, 0)
            load_adj(1, 1)
            sp.wait_ge(first_out, 16)
            sp.wait_ge(fill_out, 16)
            store_table(QB)
            sp.wait_ge(nm_out[0], 32)
            sp.wait_ge(nm_out[1], 32)
            sp.dma_start(nm_q[:, :, :], quad(nmask, 0)).then_inc(nm_in, 16)

            def step(s, lo, stages):
                a = s - LAG
                if "gather" in stages:
                    if lo > 0:
                        sp.wait_ge(x1_made, T * s)
                        sp.nop(nofuse=True)
                    sp.dma_start(h_q[:, :, :], quad(table, s % TRING)).then_inc(h_in, 16)
                    sp.dma_start(x_q[:, :, :], quad(x_r, s)).then_inc(x_in, 16)
                if "attend" in stages:
                    sp.dma_start(o_q[:, :, :], quad(xmid, a)).then_inc(x1_in, 16)
                if "index" in stages:
                    load_adj(s + 1, 2)
                    load_adj(s + 1, 3)
                if "table_rows" in stages:
                    store_table(s - 1 + AHEAD)
                if "table" in stages:
                    load_x_ln(s + AHEAD)
                if "load_index" in stages:
                    load_adj(s + 2, 0)
                    load_adj(s + 2, 1)
                if "more" in stages:
                    sp.wait_ge(pen_made, NJ * (a + 1))
                    sp.nop(nofuse=True)
                    for u in range(2):
                        sp.wait_ge(nm_out[u], 16 * 2 * (a + 2))
                        sp.nop(nofuse=True)
                    sp.dma_start(nm_q[:, :, :], quad(nmask, a + 1)).then_inc(nm_in, 16)
                if "attend" in stages:
                    sp.wait_ge(out_made, a + 2)
                    sp.nop(nofuse=True)
                    sp.dma_start(quad(out_r, a), o_q[:, :, :]).then_inc(out_out, 16)
                if "gather" in stages:
                    sp.wait_ge(x1_made, T * s + T)
                    sp.nop(nofuse=True)
                    sp.dma_start(quad(xmid, s), x1_q[:, :, :]).then_inc(x1_out, 16)
                if "attend" in stages:
                    sp.wait_ge(out_out, 16 * (a + 1))
                    sp.nop(nofuse=True)
                if "gather" in stages:
                    sp.wait_ge(x1_out, 16 * (s + 1))
                    sp.nop(nofuse=True)

            schedule(sp, step)
            sp.wait_ge(zero_out, 16)
            sp.wait_ge(table_out, 16 * (QUADS - QB))
            sp.wait_ge(nm_out[0], 16 * 2 * QUADS)
            sp.wait_ge(nm_out[1], 16 * 2 * QUADS)
            sp.wait_ge(x1_out, 16 * QUADS)
            sp.wait_ge(out_out, 16 * QUADS)

        @block.gpsimd
        def _(pool):
            pool.wait_ge(zero_out, 16)
            pool.wait_ge(first_out, 16)
            pool.wait_ge(fill_out, 16)

            def step(s, lo, stages):
                if "gather" not in stages:
                    return
                if lo > 0:
                    pool.wait_ge(table_out, 16 * s if "table" in stages else 16 * (QUADS - QB))
                for t in range(T):
                    if t % 2 == 0:
                        pool.wait_ge(idx_ready, 2 * s + t // 2 + 1)
                    pool.wait_ge(agg_made, T * s + t + 1)
                    pool.nop(nofuse=True)
                    for k in range(S):
                        pool.indirect_dma_start(
                            out=near[:, t % 2, k, :], out_offset=None, in_=table,
                            in_offset=bass.IndirectOffsetOnAxis(ap=idx[:, t, k:k + 1], axis=0),
                        ).then_inc(near_in[t % 2], 16)

            schedule(pool, step)

        @block.scalar
        def _(act):
            b1 = bank1_uses()
            act.wait_ge(cst_in, 16)
            nc.scalar.activation(ident_b[:, :], ident, ACT.Copy)
            nc.scalar.activation(neg_ident[:, :], ident, ACT.Copy, scale=-1.0)
            nc.scalar.activation(pack_w[:, :], cst[:, C_PK:C_PK + P // GB], ACT.Copy).then_inc(set_act, 1)

            def setup_weights():
                act.wait_ge(set_pe, 1)
                nc.scalar.activation(w1_t[:, :, 0:C], bank1[:, :].rearrange("p (k c) -> p k c", k=KC),
                                     ACT.Copy).then_inc(set_act, 1)
                act.wait_ge(set_pe, 2)
                nc.scalar.activation(a_t[:, :, :], bank1[:, 0:2 * KC].rearrange("p (k c) -> p k c", k=KC),
                                     ACT.Copy).then_inc(set_act, 1)
                act.wait_ge(set_pe, 3)
                nc.scalar.activation(w1_t[:, :, C:C + 2], bank1[:, 0:2 * KC].rearrange("p (k c) -> p k c", k=KC),
                                     ACT.Copy).then_inc(set_act, 1)
                act.wait_ge(set_pe, 4)
                nc.scalar.activation(bias_b[:, :], bank1[:, 0:C], ACT.Copy)
                act.wait_ge(set_act, 4)
                act.wait_ge(set_done, 2)
                for k in range(KC):
                    ins = nc.scalar.activation(wa2_b[:, k, :], ones_f[:, :], ACT.Copy,
                                               scale=w1_t[:, k, C + 1:C + 2])
                ins.then_inc(set_act, 1)

            def index_masks(q, pair, first):
                for u in range(2):
                    t = 2 * pair + u
                    act.wait_ge(adj_in[u], 16 * (2 * q + pair + 1))
                    if not (first and pair == 0):
                        act.wait_ge(nm_out[u], 16 * (2 * q + pair))
                    nc.scalar.activation(nm_t[:, u, :], adj_i[:, u, :], ACT.Relu, bias=BIG_B, scale=-BIG
                                         ).then_inc(nm_made, 1)
                for u in range(2):
                    t = 2 * pair + u
                    act.wait_ge(nm_made, T * q + t + 1)
                    act.dma_start(tile(nmask, q, t), nm_t[:, u, :]).then_inc(nm_out[u], 16)

            def index_half(q, pair, half, first):
                h = 4 * pair + half
                act.wait_ge(b1_full, b1.next())
                if not (first and h < 2):
                    act.wait_ge(packed, 2 * T * q + h - 1)
                nc.scalar.activation(nm_x[:, half % 2, :], bank1_b[:, :], ACT.Copy).then_inc(nmx_made, 1)
                act.wait_ge(nmx_made, 2 * T * q + h + 1)
                act.sem_inc(b1_free, 1)

            def normalise(q, first_col, src, dst, ready, made):
                act.wait_ge(ready, q + 1)
                for t in range(T):
                    c = first_col + t
                    nc.scalar.activation(dst[:, t, :], src[:, t, :], ACT.Relu, bias=shift[:, c:c + 1],
                                         scale=rstd[:, c:c + 1]).then_inc(made, 1)

            def project(q):
                normalise(q, T, x1_q, h2_q, ln2_ready, h2_made)
                act.wait_ge(proj_pe, 2 * q + 1)
                nc.scalar.activation(h2_t[:, :, :], acc[:, 0:KC, :], ACT.Copy).then_inc(h2t_made, 1)
                act.wait_ge(b1_full, b1.next())
                nc.scalar.activation(a2_all[:, bass.ds((q % RING) * QR, QR)], bank1[:, :], ACT.Copy
                                     ).then_inc(b1_free, 1)

            def hidden(q):
                act.wait_ge(proj_pe, 2 * q + 2)
                nc.scalar.activation(hid[:, bass.ds((q % RING) * T, T), 1:C + 3], acc[:, :, 0:C + 2], ACT.Copy
                                     ).then_inc(hid_made, 1)

            def leaky(a, c):
                for j in (2 * c, 2 * c + 1):
                    act.wait_ge(arg_made, NJ * a + j + 1)
                    nc.scalar.activation(lin[:, j % 2, :], a1_b[:, :], ACT.Relu, bias=a2_rise[:, j:j + 1],
                                         scale=RISE).then_inc(lin_made, 1)

            def chunk(a, c):
                if c + 1 < NJ // 2:
                    leaky(a, c + 1)
                act.wait_ge(arg_made, NJ * a + 2 * c + 4)
                nc.scalar.activation(wgt[:, c % 2, :], wgt[:, c % 2, :], ACT.Exp).then_inc(wgt_made, 1)

            def cat_copy():
                act.wait_ge(b1_full, b1.next())
                nc.scalar.activation(cat_t, bank1[:, :], ACT.Copy).then_inc(b1_free, 1)

            def step(s, lo, stages):
                b1.start(s, lo)
                a = s - LAG

                def attended(c, half=None):
                    if "attend" in stages:
                        chunk(a, c)
                    if "index" in stages and half is not None:
                        index_half(s + 1, 1, half, False)

                def gathered():
                    if "gather" in stages:
                        cat_copy()

                if "index" in stages:
                    index_masks(s + 1, 0, False)
                    for half in range(4):
                        index_half(s + 1, 0, half, False)
                if "project" in stages:
                    project(s - 1)
                if "attend" in stages:
                    act.wait_ge(b1_free, b1.n + 1)
                    act.wait_ge(out_made, a + 1)
                    nc.scalar.activation(a2_row, a2_all[:, bass.ds((a % RING) // QB * N, N)], ACT.Copy
                                         ).then_inc(a2_made, 1)
                if "project" in stages:
                    hidden(s - 1)
                if "table_rows" in stages:
                    normalise(s, 0, x_ln, h_ln, ln1_ready, h_made)
                gathered()
                if "index" in stages:
                    index_masks(s + 1, 1, False)
                if "attend" in stages:
                    act.wait_ge(b1_full, b1.next())
                    nc.scalar.activation(a1_b[:, :], bank1[:, :], ACT.Copy).then_inc(b1_free, 1)
                    act.wait_ge(b1_full, b1.next())
                    nc.scalar.activation(m_r[:, :], bank1_b[0:3, 0:QR], ACT.Copy).then_inc(b1_free, 1)
                    act.wait_ge(b1_free, b1.n + 1)
                    leaky(a, 0)
                gathered()
                for c in range(4):
                    attended(c, c)
                gathered()
                for c in range(4, 8):
                    attended(c)
                gathered()

            act.sem_inc(b1_free, 1)
            act.wait_ge(set_done, 3)
            BIG_B = big_c[:, :]
            b1.start(-1, -1)
            index_masks(0, 0, True)
            for half in range(4):
                index_half(0, 0, half, True)
            act.wait_ge(first_ready, 1)
            for t in range(NJ):
                nc.scalar.activation(h_first[:, t, :], x_first[:, t, :], ACT.Relu, bias=shift[:, t:t + 1],
                                     scale=rstd[:, t:t + 1]).then_inc(first_made, 1)
            index_masks(0, 1, True)
            for half in range(4):
                index_half(0, 1, half, True)
            normalise(0, 0, x_ln, h_ln, ln1_ready, h_made)
            setup_weights()
            schedule(act, step)

        @block.vector
        def _(dve):
            b2 = bank2_uses()

            nc.vector.memset(agg[:, :], 0.0).then_inc(set_done, 1)
            nc.vector.memset(ones_f[:, :], 1.0).then_inc(set_done, 1)
            nc.vector.memset(big_c[:, :], BIG).then_inc(set_done, 1)
            nc.vector.memset(ones_b[:, :], 1.0)
            nc.vector.memset(hid[:, :, 0:1], 1.0)
            dve.wait_ge(cst_in, 16)
            nc.vector.tensor_copy(pow_i[:, :], cst[:, C_POW:C_POW + GB]).then_inc(set_done, 1)
            dve.wait_ge(set_done, 4)
            dve.sem_inc(agg_made, 2)
            dve.sem_inc(b2_free, 1)
            dve.sem_inc(arg_made, 2)
            dve.sem_inc(out_made, 1)
            dve.wait_ge(zero_out, 16)

            def statistics(cols, sources, ready):
                lo, hi = cols
                chain, cnt = ln_step, Count()
                for c, src in sources:
                    ins = nc.vector.bn_stats(stat[:, c, :], src)
                ins.then_inc(chain, 1)
                dve.wait_ge(chain, cnt.next())
                for c, _ in sources:
                    ins = nc.vector.bn_aggr(mv[:, c, :], stat[:, c, :])
                ins.then_inc(chain, 1)
                dve.wait_ge(chain, cnt.next())
                v, y, n = var[:, lo:hi], rstd[:, lo:hi], nwt[:, lo:hi]
                nc.vector.tensor_scalar(v, mv[:, lo:hi, 1], EPS, None, ALU.add).then_inc(chain, 1)
                dve.wait_ge(chain, cnt.next())
                nc.vector.tensor_scalar(rsq_i[:, lo:hi], v.bitcast(I32), 1, None, ALU.arith_shift_right
                                        ).then_inc(chain, 1)
                dve.wait_ge(chain, cnt.next())
                nc.vector.tensor_scalar(y.bitcast(I32), rsq_i[:, lo:hi], -1.0, float(0x5F3759DF), ALU.mult, ALU.add
                                        ).then_inc(chain, 1)
                dve.wait_ge(chain, cnt.next())
                for _ in range(3):
                    nc.vector.tensor_tensor(n, y, y, ALU.mult).then_inc(chain, 1)
                    dve.wait_ge(chain, cnt.next())
                    nc.vector.scalar_tensor_tensor(n, n, -0.5, v, ALU.mult, ALU.mult).then_inc(chain, 1)
                    dve.wait_ge(chain, cnt.next())
                    nc.vector.scalar_tensor_tensor(y, n, 1.5, y, ALU.add, ALU.mult).then_inc(chain, 1)
                    dve.wait_ge(chain, cnt.next())
                nc.vector.scalar_tensor_tensor(shift[:, lo:hi], mv[:, lo:hi, 0], -1.0, y, ALU.mult, ALU.mult
                                               ).then_inc(ready, 1)
                dve.sem_clear(chain)

            def table_alone():
                dve.wait_ge(xln_in, 16)
                dve.wait_ge(first_made, NJ)
                statistics((0, T), [(t, x_ln[:, t, :]) for t in range(T)], ln1_ready)

            def statistics_of_step(s, stages):
                dve.wait_ge(x1_made, T * s + T)
                if "table" in stages:
                    dve.wait_ge(xln_in, 16 * (s + 2))
                    cols, src = (0, 2 * T), [(t, x_ln[:, t, :]) for t in range(T)]
                else:
                    cols, src = (T, 2 * T), []
                src = src + [(T + t, x1_q[:, t, :]) for t in range(T)]
                statistics(cols, src, ln2_ready)
                if "table" in stages:
                    dve.wait_ge(ln2_ready, s + 1)
                    dve.sem_inc(ln1_ready, 1)

            def top_rounds(src, ix_n):
                for r in range(TOP // 8):
                    seen = []
                    for u in range(2):
                        if r > 0:
                            dve.wait_ge(ix_step, gone[u])
                        nc.vector.max(top[:, u, 8 * r:8 * r + 8], src[:, u, :]).then_inc(ix_step, 1)
                        seen.append(ix_n.next())
                    gone = []
                    if r < TOP // 8 - 1:
                        for u in range(2):
                            dve.wait_ge(ix_step, seen[u])
                            nc.vector.match_replace(src[:, u, :], top[:, u, 8 * r:8 * r + 8], src[:, u, :], PADKEY
                                                    ).then_inc(ix_step, 1)
                            gone.append(ix_n.next())
                dve.wait_ge(ix_step, seen[1])

            def index_words(q):
                words = bank2[:, :].rearrange("p (u g) -> p u g", u=2)
                dve.wait_ge(b2_full, b2.next())
                base = word_base.unsqueeze(1).to_broadcast([P, 2, NG])
                nc.vector.scalar_tensor_tensor(key2[:, :, :], words, -(2.0 ** GB - 1.5), base, ALU.is_gt, ALU.mult
                                               ).then_inc(ix_step, 1)
                dve.wait_ge(ix_step, 1)
                nc.vector.tensor_tensor(key[:, :, :], key2[:, :, :], words, ALU.add).then_inc(b2_free, 1)
                nc.vector.tensor_copy(code[:, :], cst[:, bass.ds(q * 2 + C_CODE, 2)]).then_inc(ix_step, 1)

            def index_rest(q, pair, between):
                ix_n = Count(2)
                dve.wait_ge(ix_step, 2)
                top_rounds(key, ix_n)
                nc.vector.tensor_scalar(top_i[:, :], top[:, :, :].rearrange("p u k -> p (u k)"), 0.0, None, ALU.max
                                        ).then_inc(ix_step, 1)
                dve.wait_ge(ix_step, ix_n.next())
                words_i = top_i[:, :].unsqueeze(2).to_broadcast([P, 2 * TOP, GB])
                powers = pow_i[:, :].unsqueeze(1).to_broadcast([P, 2 * TOP, GB])
                nc.vector.tensor_tensor(bits[:, :].rearrange("p (k j) -> p k j", j=GB), words_i, powers,
                                        ALU.bitwise_and).then_inc(ix_step, 1)
                ix_n.next()
                nc.vector.tensor_scalar(high_i[:, :], top_i[:, :], (2 ** GB - 1) ^ 0xFFFFF, None, ALU.bitwise_and
                                        ).then_inc(ix_step, 1)
                dve.wait_ge(ix_step, ix_n.next())
                high = high_i[:, :].unsqueeze(2).to_broadcast([P, 2 * TOP, GB])
                place = cst[:, C_J:C_J + GB].unsqueeze(1).to_broadcast([P, 2 * TOP, GB])
                nc.vector.scalar_tensor_tensor(
                    key2[:, :, :].rearrange("p u (k j) -> p (u k) j", j=GB), high, GB / 2.0 ** GB, place,
                    ALU.mult, ALU.subtract).then_inc(ix_step, 1)
                dve.wait_ge(ix_step, ix_n.next())
                nc.vector.scalar_tensor_tensor(
                    key[:, :, :].rearrange("p u g -> p (u g)"), bits[:, :], 0.0,
                    key2[:, :, :].rearrange("p u g -> p (u g)"), ALU.is_gt, ALU.mult).then_inc(ix_step, 1)
                between()
                dve.wait_ge(ix_step, ix_n.next())
                top_rounds(key, ix_n)
                nc.vector.tensor_scalar(miss[:, :, :], top[:, :, :], 0.0, code[:, 1:2], ALU.is_equal, ALU.mult
                                        ).then_inc(ix_step, 1)
                dve.wait_ge(ix_step, ix_n.next())
                nc.vector.scalar_tensor_tensor(idx[:, 2 * pair:2 * pair + 2, :], miss[:, :, :], code[:, 0:1],
                                               top[:, :, :], ALU.add, ALU.subtract).then_inc(idx_ready, 1)
                dve.sem_clear(ix_step)

            def maximum(s, t):
                dve.wait_ge(near_in[t % 2], 16 * S * (2 * s + t // 2 + 1))
                nc.vector.tensor_reduce(agg[:, :], near[:, t % 2, :, :].rearrange("p k c -> p c k"), AX.X, ALU.max
                                        ).then_inc(agg_made, 1)

            def residual0(s, t, lo):
                if t == 0:
                    dve.wait_ge(x_in, 16 * (s + 1))
                    dve.wait_ge(h_in, 16 * (s + 1))
                    if lo > 0:
                        dve.wait_ge(h2_made, T * s)
                dve.wait_ge(b2_full, b2.next())
                nc.vector.scalar_tensor_tensor(x1_q[:, t, :], bank2[:, 0:C], 0.0, x_q[:, t, :], ALU.max, ALU.add
                                               ).then_inc(b2_free, 1)
                dve.wait_ge(b2_free, b2.n + 1)
                dve.sem_inc(x1_made, 1)

            def attend_setup(a, lo):
                as_n = Count()
                dve.wait_ge(nm_in, 16 * (a + 1))
                dve.wait_ge(a2_made, a + 1)
                dve.nop(nofuse=True)
                batch = (a % RING) // QB
                for t in range(T):
                    nc.vector.tensor_tensor_reduce(
                        out=junk, in0=a2_row, in1=nm_q[:, t, :], scale=1.0,
                        scalar=-3.0e38, op0=ALU.subtract, op1=ALU.max, accum_out=amax[:, t:t + 1]
                        ).then_inc(as_step, 1)
                    dve.wait_ge(as_step, as_n.next())
                dve.wait_ge(hid_made, a + LAG if lo < QUADS else QUADS)
                nc.vector.tensor_scalar(a2_rise[:, :], hid[:, bass.ds(batch * NJ, NJ), C + 2], RISE, None, ALU.mult)
                nc.vector.tensor_scalar(a2_slope[:, :], hid[:, bass.ds(batch * NJ, NJ), C + 2], SLOPE, None, ALU.mult)
                nc.vector.tensor_copy(a1_c[:, :], hid[:, bass.ds((a % RING) * T, T), C + 1]).then_inc(as_step, 1)
                as_n.next()
                nc.vector.tensor_scalar(lone[:, :], amax[:, :], -BIG / 2, None, ALU.is_lt).then_inc(as_step, 1)
                lone_n = as_n.next()
                nc.vector.scalar_tensor_tensor(cmax[:, :], amax[:, :], -BIG / 2, amax[:, :], ALU.is_ge, ALU.mult
                                               ).then_inc(as_step, 1)
                as_n.next()
                dve.wait_ge(as_step, lone_n)
                nc.vector.scalar_tensor_tensor(a1_p[:, :], lone[:, :], FAR, a1_c[:, :], ALU.mult, ALU.add
                                               ).then_inc(as_step, 1)
                dve.wait_ge(as_step, as_n.next())
                nc.vector.tensor_tensor(diag, ident.unsqueeze(1).to_broadcast([P, T, P]),
                                        a1_p[:, :].unsqueeze(2).to_broadcast([P, T, P]), ALU.mult
                                        ).then_inc(diag_made, 1)
                nc.vector.tensor_tensor(rest[:, :], a1_c[:, :], cmax[:, :], ALU.add).then_inc(as_step, 1)
                dve.wait_ge(as_step, as_n.next())
                nc.vector.scalar_tensor_tensor(rmax[:, :], rest[:, :], SLOPE, rest[:, :], ALU.mult, ALU.max
                                               ).then_inc(as_step, 1)
                dve.wait_ge(as_step, as_n.next())
                nc.vector.scalar_tensor_tensor(rest[:, :], a1_c[:, :], SLOPE, rmax[:, :], ALU.mult, ALU.subtract
                                               ).then_inc(as_step, 1)
                dve.wait_ge(as_step, as_n.next())
                nc.vector.scalar_tensor_tensor(nmax[:, :], lone[:, :], LONE, rest[:, :], ALU.mult, ALU.add
                                               ).then_inc(as_step, 1)
                dve.wait_ge(as_step, as_n.next())
                nc.vector.tensor_copy(m_c[:, :, 0], nmax[:, :]).then_inc(as_step, 1)
                dve.wait_ge(as_step, as_n.next())
                nc.vector.tensor_tensor(rest[:, :], nmax[:, :], m_c[:, :, 0], ALU.subtract).then_inc(as_step, 1)
                dve.wait_ge(as_step, as_n.next())
                nc.vector.tensor_copy(m_c[:, :, 1], rest[:, :]).then_inc(as_step, 1)
                dve.wait_ge(as_step, as_n.next())
                nc.vector.tensor_tensor(m_c[:, :, 2], rest[:, :], m_c[:, :, 1], ALU.subtract).then_inc(m_made, 1)
                dve.sem_clear(as_step)

            def chunk(a, c):
                dve.wait_ge(wgt_used, NJ // 2 * a + c + 1)
                for i in range(2):
                    j = 2 * c + i
                    dve.wait_ge(pen_made, NJ * a + j + 1)
                    dve.wait_ge(lin_made, NJ * a + j + 1)
                    nc.vector.scalar_tensor_tensor(wgt[:, c % 2, i * QR:(i + 1) * QR], pen[:, j % 2, :],
                                                   a2_slope[:, j:j + 1], lin[:, j % 2, :], ALU.add, ALU.add
                                                   ).then_inc(arg_made, 1)

            def attend_end(a):
                af_n = Count()
                dve.wait_ge(wgt_used, NJ // 2 * (a + 1) + 2)
                dve.wait_ge(x1_in, 16 * (a + 1))
                nc.vector.reciprocal(rden[:, :], acc[:, :, 0]).then_inc(af_step, 1)
                dve.wait_ge(af_step, af_n.next())
                for t in range(T):
                    ins = nc.vector.scalar_tensor_tensor(near_out[:, t, :], acc[:, t, 1:C + 1], rden[:, t:t + 1],
                                                         bias_b[:, :], ALU.mult, ALU.add)
                ins.then_inc(af_step, 1)
                dve.wait_ge(af_step, af_n.next())
                nc.vector.tensor_tensor(o_q[:, :, :], near_out[:, :, :], o_q[:, :, :], ALU.add).then_inc(out_made, 1)
                dve.sem_clear(af_step)

            def step(s, lo, stages):
                b2.start(s, lo)
                a = s - LAG

                def attended(*chunks):
                    if "attend" in stages:
                        for c in chunks:
                            chunk(a, c)

                def gathered(t):
                    if "gather" in stages:
                        maximum(s, t)

                def finished(t):
                    if "gather" in stages:
                        residual0(s, t, lo)

                if "index" in stages:
                    index_words(s + 1)
                gathered(0)
                if "attend" in stages:
                    attend_setup(a, lo)
                finished(0)
                gathered(1)
                attended(0)
                if "index" in stages:
                    def between():
                        finished(1)
                        attended(1)
                    index_rest(s + 1, 0, between)
                else:
                    finished(1)
                    attended(1)
                attended(2, 3)
                gathered(2)
                if "index" in stages:
                    index_words(s + 1)
                attended(4)
                finished(2)
                attended(5, 6, 7)
                gathered(3)
                if "attend" in stages:
                    attend_end(a)
                finished(3)
                if "gather" in stages:
                    statistics_of_step(s, stages)
                if "index" in stages:
                    index_rest(s + 1, 1, lambda: None)

            near_out = wgt_flat[:, 0:T * C].rearrange("p (t c) -> p t c", t=T)
            b2.start(-1, -1)
            dve.wait_ge(first_in, 16)
            statistics((0, NJ), [(t, x_first[:, t, :]) for t in range(NJ)], first_ready)
            for pair in range(2):
                index_words(0)
                index_rest(0, pair, lambda: None)
            table_alone()
            schedule(dve, step)

        @block.tensor
        def _(pe):
            b1, b2 = bank1_uses(), bank2_uses()

            def setup_weights():
                pe.wait_ge(w_in, 80)
                pe.wait_ge(cst_in, 16)
                for o in range(KC):
                    for i in range(KC):
                        mm = nc.tensor.transpose(bank1[:, i * C + o * P:i * C + (o + 1) * P],
                                                 w1_n[:, o, i * P:(i + 1) * P], ident)
                mm.then_inc(set_pe, 1)
                pe.wait_ge(set_act, 2)
                for o in range(KC):
                    mm = nc.tensor.transpose(bank1[:, 2 * o:2 * o + 2], a_rows[:, o * P:(o + 1) * P], ident[0:2, 0:2])
                mm.then_inc(set_pe, 1)
                pe.wait_ge(set_act, 3)
                for i in range(KC):
                    for o in range(KC):
                        mm = nc.tensor.matmul(bank1[:, 2 * i:2 * i + 2], w1_n[:, o, i * P:(i + 1) * P], a_t[:, o, :],
                                              start=(o == 0), stop=(o == KC - 1))
                mm.then_inc(set_pe, 1)
                pe.wait_ge(set_act, 4)
                pe.wait_ge(set_done, 2)
                nc.tensor.matmul(bank1[:, 0:C], ones_f[0:1, :], bias_row, start=True, stop=True
                                 ).then_inc(set_pe, 1)
                pe.wait_ge(set_act, 5)
                pe.wait_ge(set_done, 4)
                pe.sem_inc(wgt_used, 2)

            def index_transpose(q, pair, half):
                u = half // 2
                pe.wait_ge(nm_made, T * q + 2 * pair + u + 1)
                pe.wait_ge(b1_free, b1.next())
                for i in range(NJ // 2):
                    j = half % 2 * NJ // 2 + i
                    mm = nc.tensor.transpose(bank1_b[:, i * P:(i + 1) * P], nm_t[:, u, j * P:(j + 1) * P],
                                             ident_b[:, :])
                mm.then_inc(b1_full, 1)

            def index_pack(q, pair, half):
                u = half // 2
                if half == 0:
                    pe.wait_ge(b2_free, b2.next())
                pe.wait_ge(nmx_made, 2 * T * q + 4 * pair + half + 1)
                for i in range(NJ // 2):
                    j = half % 2 * NJ // 2 + i
                    w = P // GB
                    mm = nc.tensor.matmul(bank2[:, u * NG + j * w:u * NG + (j + 1) * w],
                                          nm_x[:, half % 2, i * P:(i + 1) * P], pack_w[:, :],
                                          start=True, stop=True)
                mm.then_inc(packed, 1)
                if half == 3:
                    pe.wait_ge(packed, 2 * T * q + 4 * pair + 4)
                    pe.sem_inc(b2_full, 1)

            def index_prep(q, pair):
                index_transpose(q, pair, 0)
                for half in range(4):
                    if half < 3:
                        index_transpose(q, pair, half + 1)
                    index_pack(q, pair, half)

            def layer0(s, t):
                if t == 0:
                    pe.wait_ge(h_in, 16 * (s + 1))
                pe.wait_ge(agg_made, T * s + t + 3)
                pe.wait_ge(b1_free, b1.next())
                for k in range(KC):
                    nc.tensor.transpose(bank1[:, k * P:(k + 1) * P], h_q[:, t, k * P:(k + 1) * P], ident)
                for k in range(KC):
                    mm = nc.tensor.transpose(bank1[:, (KC + k) * P:(KC + k + 1) * P], agg[:, k * P:(k + 1) * P],
                                             ident)
                mm.then_inc(b1_full, 1)
                pe.wait_ge(b1_free, b1.n + 1)
                pe.wait_ge(b2_free, b2.next())
                for k in range(2 * KC):
                    nc.tensor.matmul(bank2[:, 0:C], cat_t[:, k * P:(k + 1) * P], w0_sb[:, k, :],
                                     start=(k == 0), stop=False)
                nc.tensor.matmul(bank2[:, 0:C], ones_f[0:1, :], b0_row[:, :], start=False, stop=True
                                 ).then_inc(b2_full, 1)

            def project(q):
                pe.wait_ge(h2_made, T * q + T)
                for k in range(KC):
                    for t in range(T):
                        mm = nc.tensor.transpose(acc[:, k, t * P:(t + 1) * P], h2_q[:, t, k * P:(k + 1) * P], ident)
                mm.then_inc(proj_pe, 1)
                pe.wait_ge(h2t_made, q + 1)
                pe.wait_ge(b1_free, b1.next())
                for k in range(KC):
                    mm = nc.tensor.matmul(bank1[:, :], wa2_b[:, k, :], h2_t[:, k, :], start=(k == 0),
                                          stop=(k == KC - 1))
                mm.then_inc(b1_full, 1)
                for t in range(T):
                    for k in range(KC):
                        mm = nc.tensor.matmul(acc[:, t, 0:C + 2], h2_t[:, k, t * P:(t + 1) * P], w1_t[:, k, :],
                                              start=(k == 0), stop=(k == KC - 1))
                mm.then_inc(proj_pe, 1)

            def attend_setup(a):
                pe.wait_ge(diag_made, a + 1)
                pe.wait_ge(b1_free, b1.next())
                nc.tensor.matmul(bank1[:, :], ones_f[:, :], lin[:, 0, :], start=True, stop=True).then_inc(b1_full, 1)
                pe.wait_ge(m_made, a + 1)
                pe.wait_ge(b1_free, b1.next())
                for t in range(T):
                    mm = nc.tensor.transpose(bank1_b[0:3, t * P:(t + 1) * P], m_c[:, t, :], ident_b[:, :])
                mm.then_inc(b1_full, 1)
                pe.wait_ge(b1_free, b1.n + 1)
                penalty(a, 0)

            def penalty(a, c):
                for j in (2 * c, 2 * c + 1):
                    pe.wait_ge(arg_made, NJ * a + j + 1)
                    nc.tensor.matmul(pen[:, j % 2, :], ones_b[:, :], m_r[:, :], start=True, stop=False,
                                     skip_group_check=True)
                    for t in range(T):
                        mm = nc.tensor.matmul(pen[:, j % 2, t * P:(t + 1) * P], nm_q[:, t, j * P:(j + 1) * P],
                                              neg_ident[:, :], start=False, stop=(t == T - 1),
                                              skip_group_check=True)
                    mm.then_inc(pen_made, 1)

            def chunk(a, c):
                if c + 1 < NJ // 2:
                    penalty(a, c + 1)
                pe.wait_ge(wgt_made, NJ // 2 * a + c + 1)
                if c == 0:
                    pe.wait_ge(out_made, a + 1)
                batch = (a % RING) // QB
                for i in range(2):
                    j = 2 * c + i
                    for t in range(T):
                        mm = nc.tensor.matmul(
                            acc[:, t, 0:C + 1], wgt[:, c % 2, i * QR + t * P:i * QR + (t + 1) * P],
                            hid[:, bass.ds(batch * NJ + j, 1), 0:C + 1].rearrange("p a c -> p (a c)"),
                            start=(j == 0), stop=(j == NJ - 1), skip_group_check=True)
                mm.then_inc(wgt_used, 1)

            def step(s, lo, stages):
                b1.start(s, lo)
                b2.start(s, lo)
                a = s - LAG

                def gathered(t):
                    if "gather" in stages:
                        layer0(s, t)

                if "index" in stages:
                    index_prep(s + 1, 0)
                if "project" in stages:
                    project(s - 1)
                gathered(0)
                if "attend" in stages:
                    attend_setup(a)
                gathered(1)
                if "index" in stages:
                    index_transpose(s + 1, 1, 0)
                for c in range(4):
                    if "attend" in stages:
                        chunk(a, c)
                    if "index" in stages:
                        if c < 3:
                            index_transpose(s + 1, 1, c + 1)
                        index_pack(s + 1, 1, c)
                gathered(2)
                for c in range(4, 8):
                    if "attend" in stages:
                        chunk(a, c)
                gathered(3)

            b1.start(-1, -1)
            b2.start(-1, -1)
            pe.wait_ge(set_act, 1)
            index_prep(0, 0)
            index_prep(0, 1)
            pe.wait_ge(b1_free, b1.n + 1)
            setup_weights()
            schedule(pe, step)


_INS = ["x", "adj", "L0_gnn_W", "L0_gnn_b", "L1_gnn_W", "L1_gnn_a", "L1_gnn_bias"]


def kernel(**inputs):
    import concourse.bacc as _bacc
    from concourse.bass_utils import run_bass_kernel_spmd as _run

    nc = _bacc.Bacc("TRN2", target_bir_lowering=False, num_devices=1)
    arrays, args = {}, []
    laid_out = [(name, np.ascontiguousarray(inputs[name])) for name in _INS] + [("consts", shape_constants())]
    for name, a in laid_out:
        arrays[f"in_{name}_dram"] = a
        args.append(nc.dram_tensor(f"in_{name}_dram", a.shape, mybir.dt.from_np(a.dtype), kind="ExternalInput").ap())
    out = nc.dram_tensor("out_0_dram", (B, N, C), F32, kind="ExternalOutput").ap()
    table = nc.dram_tensor("table_dram", (ZERO_ROW + 1, C), F32, kind="Internal").ap()
    xmid = nc.dram_tensor("xmid_dram", (ROWS, C), F32, kind="Internal").ap()
    nmask = nc.dram_tensor("nmask_dram", (ROWS, N), BF16, kind="Internal").ap()
    two_layers(nc, *args, out, table, xmid, nmask)
    r = _run(nc, [arrays], core_ids=[0])
    return r.results[0]["out_0_dram"]
```

```python
from contextlib import ExitStack

import numpy as np

import concourse.bass as bass
from concourse import mybir

ALU = mybir.AluOpType
ACT = mybir.ActivationFunctionType
AX = mybir.AxisListType
BF16 = mybir.dt.bfloat16
F32 = mybir.dt.float32
I32 = mybir.dt.int32

P = 128
B, N, C = 8, 2048, 256
S = 25
T = 4
QR = T * P
ROWS = B * N
QUADS = ROWS // QR
QB = N // QR
NJ = N // P
LAG = QB
AHEAD = QB + 1
TRING = 2 * QB
RING = 2 * QB
GB = 8
NG = N // GB
TOP = 32
HW = C + 4
KC = C // P
EPS = 1e-5
SLOPE = 0.2
BIG = float(2 ** 40)
RISE = 1.0 - SLOPE
FAR = float(2 ** 60)
LONE = BIG - float(np.float32(RISE)) * FAR
PADKEY = -1000.0
ZERO_ROW = TRING * QR

C_ID, C_BASE, C_J, C_POW, C_PK, C_CODE = 0, P, P + NG, P + NG + GB, P + NG + 2 * GB, P + NG + 2 * GB + P // GB
C_ALL = C_CODE + 2 * QUADS

STEPS = {
    "index": (-1, QUADS - 2),
    "load_index": (0, QUADS - 3),
    "table": (0, QUADS - 1 - AHEAD),
    "table_rows": (1, QUADS - AHEAD),
    "gather": (0, QUADS - 2),
    "project": (1, QUADS - 2),
    "attend": (LAG, QUADS - 2),
}


LAST = QUADS - 1
KNOWN = (QB - 1) * (T // 2)
TASKS = [(LAST - 4, 0, NJ // 2), (LAST - 3, 0, KNOWN), (LAST - 2, 0, KNOWN),
         (LAST - 3, KNOWN, NJ // 2 - KNOWN), (LAST - 1, 0, NJ // 2),
         (LAST - 2, KNOWN, NJ // 2 - KNOWN), (LAST, 0, NJ // 2)]
FINISHED = [LAST - 4, LAST - 3, LAST - 1, LAST - 2, LAST]
TASK_AT = [NJ // 2 * (LAST - 4) + sum(n for _, _, n in TASKS[:k]) for k in range(len(TASKS))]


def shape_constants():
    c = np.zeros((P, C_ALL), np.float32)
    c[:, C_ID:C_ID + P] = np.eye(P)
    c[:, C_BASE:C_BASE + NG] = (NG - np.arange(NG)) * 2.0 ** GB + (2.0 ** GB - 1)
    c[:, C_J:C_J + GB] = np.arange(GB)
    c[:, C_POW:C_POW + GB] = 2.0 ** np.arange(GB)
    for m in range(P):
        c[m, C_PK + m // GB] = -(2.0 ** (m % GB)) / BIG
    for q in range(QUADS):
        base = N * (q // QB % (TRING // QB) + 1)
        c[:, C_CODE + 2 * q] = base
        c[:, C_CODE + 2 * q + 1] = ZERO_ROW - base
    return c


class Uses:

    def __init__(self, **per_step):
        self.per_step = per_step
        self.n = 0

    def start(self, s, lo):
        self.n = 0
        for kind, uses in self.per_step.items():
            first, last = STEPS[kind]
            if lo > last:
                self.n = self.n + uses * (last - first + 1)
            elif lo >= first:
                self.n = self.n + (s - first) * uses

    def next(self):
        self.n = self.n + 1
        return self.n


class Count:

    def __init__(self, done=0):
        self.k = done

    def next(self):
        self.k += 1
        return self.k


def bank1_uses():
    return Uses(attend=2, gather=T, index=4 * T // 2, project=1)


def bank2_uses():
    return Uses(gather=T, index=2)


def two_layers(nc, x, adj, w0, b0, w1, a1, bias1, consts, out, table, xmid, nmask):
    rows = lambda ap: ap.rearrange("b n c -> (b n) c")
    x_r, adj_r, out_r = rows(x), rows(adj), rows(out)
    quad = lambda ap, q: ap[bass.ds(q * QR, QR), :].rearrange("(t p) c -> p t c", p=P)
    tile = lambda ap, q, t: ap[bass.ds(q * QR + t * P, P), :]

    with ExitStack() as ctx:
        def sb(name, shape, dt):
            return ctx.enter_context(nc.sbuf_tensor(name, shape, dt))

        def psum(name, shape, dt):
            return ctx.enter_context(nc.psum_tensor(name, shape, dt))

        def sem(name):
            return ctx.enter_context(nc.semaphore(name))

        cst = sb("cst", [P, C_ALL], F32)
        ident_b = sb("ident_b", [P, P], BF16)
        neg_ident = sb("neg_ident", [P, P], BF16)
        pack_w = sb("pack_w", [P, P // GB], BF16)
        pow_i = sb("pow_i", [P, GB], I32)
        ones_f = sb("ones_f", [P, P], F32)
        ones_b = sb("ones_b", [3, P], BF16)
        w0_sb = sb("w0_sb", [P, 2 * KC, C], F32)
        b0_row = sb("b0_row", [1, C], F32)
        bias_b = sb("bias_b", [P, C], F32)
        w1_t = sb("w1_t", [P, KC, C + 2], F32)
        wa2_b = sb("wa2_b", [P, KC, P], F32)
        a_t = sb("a_t", [P, KC, 2], F32)
        ident = cst[:, C_ID:C_ID + P]
        word_base = cst[:, C_BASE:C_BASE + NG]

        near = sb("near", [P, 2, S, C], F32)
        hid = sb("hid", [P, RING * T, HW], F32)
        a2_all = sb("a2_all", [P, RING * QR], F32)
        a1_b = sb("a1_b", [P, QR], F32)
        nm_q = sb("nm_q", [P, T, N], BF16)
        adj_i = sb("adj_i", [P, 2, N], I32)
        nm_t = sb("nm_t", [P, 2, N], BF16)
        nm_x = sb("nm_x", [P, 2, N // 2], BF16)
        lin = sb("lin", [P, 2, QR], F32)
        wgt = sb("wgt", [P, 2, 2 * QR], F32)
        x_ln = sb("x_ln", [P, T, C], F32)
        h_ln = sb("h_ln", [P, T, C], F32)
        h_q = sb("h_q", [P, T, C], F32)
        x_q = sb("x_q", [P, T, C], F32)
        x1_q = sb("x1_q", [P, T, C], F32)
        h2_t = sb("h2_t", [P, KC, QR], F32)
        o_q = sb("o_q", [P, T, C], F32)
        agg = sb("agg", [P, C], F32)
        key = sb("key", [P, 2, NG], F32)
        key2 = sb("key2", [P, 2, NG], F32)
        bits = sb("bits", [P, 2 * NG], I32)
        top = sb("top", [P, 2, TOP], F32)
        top_i = sb("top_i", [P, 2 * TOP], I32)
        high_i = sb("high_i", [P, 2 * TOP], I32)
        code = sb("code", [P, 2], F32)
        big_c = sb("big_c", [P, 1], F32)
        miss = sb("miss", [P, 2, TOP], F32)
        idx = sb("idx", [P, T, TOP], I32)
        stat = sb("stat", [P, NJ, 6], F32)
        mv = sb("mv", [P, NJ, 2], F32)
        var = sb("var", [P, NJ], F32)
        rsq_i = sb("rsq_i", [P, NJ], I32)
        rstd = sb("rstd", [P, NJ], F32)
        nwt = sb("nwt", [P, NJ], F32)
        shift = sb("shift", [P, NJ], F32)
        a2_rise = sb("a2_rise", [P, NJ], F32)
        a2_slope = sb("a2_slope", [P, NJ], F32)
        a1_c = sb("a1_c", [P, T], F32)
        amax = sb("amax", [P, T], F32)
        lone = sb("lone", [P, T], F32)
        cmax = sb("cmax", [P, T], F32)
        a1_p = sb("a1_p", [P, T], F32)
        rmax = sb("rmax", [P, T], F32)
        nmax = sb("nmax", [P, T], F32)
        rest = sb("rest", [P, T], F32)
        m_c = sb("m_c", [P, T, 3], BF16)
        m_r = sb("m_r", [3, QR], BF16)
        rden = sb("rden", [P, T], F32)
        amax_q = sb("amax_q", [P, QB, T], F32)
        nmax_p = sb("nmax_p", [P, 2, T], F32)
        sum_p = sb("sum_p", [P, 2, T], F32)
        scale_p = sb("scale_p", [P, 2, T], F32)
        acc = psum("acc", [P, T, 512], F32)
        pen = psum("pen", [P, 2, 512], F32)
        bank1 = psum("bank1", [P, 512], F32)
        bank2 = psum("bank2", [P, 512], F32)
        bank1_b = bank1[:, :].bitcast(BF16)

        wgt_flat = wgt[:, :, :].rearrange("p a b -> p (a b)")
        h2_q = wgt_flat[:, 0:T * C].rearrange("p (t c) -> p t c", t=T)
        a2_row = wgt_flat[:, 0:N]
        junk = lin[:, :, :].rearrange("p a b -> p (a b)").bitcast(BF16)
        x_first = near[:, 0, 0:NJ, :]
        h_first = near[:, 1, 0:NJ, :]
        near_b = near[:, :, :, :].rearrange("p a k c -> p (a k c)").bitcast(BF16)[:, 0:2 * T * N]
        nm_near = near_b.rearrange("p (t n) -> p t n", n=N)
        nm_adj = adj_i[:, :, :].rearrange("p a n -> p (a n)").bitcast(BF16).rearrange("p (t n) -> p t n", n=N)
        nm_of = {LAST - 4: nm_q[:, :, :], LAST - 3: nm_adj, LAST - 2: nm_q[:, :, :],
                 LAST - 1: nm_near[:, 0:T, :], LAST: nm_near[:, T:2 * T, :]}
        nm_x_f = nm_x[:, :, :].rearrange("p a n -> p (a n)").bitcast(F32)
        key_f = key[:, :, :].rearrange("p u g -> p (u g)")
        key2_b = key2[:, :, :].rearrange("p u g -> p (u g)").bitcast(BF16)
        a1_rows = [a1_b[:, :], nm_x_f[:, 0:QR], key_f[:, 0:QR]]
        diag_last = nm_x_f[:, QR:2 * QR]
        m_rows = [m_r[:, :], nm_t[0:3, 1, 0:QR], key2_b[0:3, 0:QR]]
        junk_last = nm_t[:, 0, :]
        part = {LAST - 3: x_ln, LAST - 2: h_ln}
        a2_of = lambda a: a2_all[:, a % RING // QB * N:(a % RING // QB + 1) * N]
        diag = lin[:, 0, :].rearrange("p (t c) -> p t c", t=T)
        w1_n = wgt_flat[:, 0:KC * C].rearrange("p (k c) -> p k c", k=KC)
        bias_row = wgt_flat[0:1, KC * C:KC * C + C]
        a_rows = wgt_flat[0:2, KC * C + C:KC * C + 2 * C]
        cat_t = h2_t[:, 0, :]
        zeros = agg[0:1, :]

        cst_in, w_in = sem("cst_in"), sem("w_in")
        first_in = [sem(f"first_in{i}") for i in range(QB)]
        first_out = sem("first_out")
        xln_in, h_in, x_in, x1_in = sem("xln_in"), sem("h_in"), sem("x_in"), sem("x1_in")
        adj_in = [sem("adj_in0"), sem("adj_in1")]
        nm_in = sem("nm_in")
        near_in = [sem("near_in0"), sem("near_in1")]
        zero_out, table_out, x1_out, out_out = sem("zero_out"), sem("table_out"), sem("x1_out"), sem("out_out")
        fill_out = sem("fill_out")
        nm_out = [sem("nm_out0"), sem("nm_out1")]
        set_done = sem("set_done")
        set_act = sem("set_act")
        set_pe = sem("set_pe")
        b1_full, b1_free = sem("b1_full"), sem("b1_free")
        b2_full, b2_free = sem("b2_full"), sem("b2_free")
        ix_step = sem("ix_step")
        idx_ready = sem("idx_ready")
        nm_made = sem("nm_made")
        nmx_made = sem("nmx_made")
        packed = sem("packed")
        agg_made = sem("agg_made")
        x1_made = sem("x1_made")
        ln_step = sem("ln_step")
        ln1_ready, ln2_ready = sem("ln1_ready"), sem("ln2_ready")
        h_made = sem("h_made")
        first_ready, first_made = sem("first_ready"), sem("first_made")
        h2_made = sem("h2_made")
        proj_pe = sem("proj_pe")
        h2t_made = sem("h2t_made")
        hid_made = sem("hid_made")
        a2_made = sem("a2_made")
        as_step = sem("as_step")
        diag_made, m_made = sem("diag_made"), sem("m_made")
        pen_made = sem("pen_made")
        lin_made = sem("lin_made")
        arg_made = sem("arg_made")
        wgt_made = sem("wgt_made")
        wgt_used = sem("wgt_used")
        af_step = sem("af_step")
        nm_adj_in, nm_near_in = sem("nm_adj_in"), sem("nm_near_in")
        acc_read = sem("acc_read")
        cols_made = sem("cols_made")
        dist_made = sem("dist_made")
        scale_made = sem("scale_made")
        out_made = sem("out_made")

        block = ctx.enter_context(nc.Block())

        def schedule(engine, step):
            edges = sorted({s for first, last in STEPS.values() for s in (max(first, 0), last + 1)})
            for lo, hi in zip(edges, edges[1:]):
                stages = {kind for kind, (first, last) in STEPS.items() if first <= lo <= last}
                if hi - lo == 1:
                    step(lo, lo, stages)
                else:
                    with engine.Fori(lo, hi) as s:
                        step(s, lo, stages)

        @block.sync
        def _(sp):
            sp.dma_start(cst[:, :], consts).then_inc(cst_in, 16)
            for i in range(QB):
                sp.dma_start(x_first[:, i * T:(i + 1) * T, :], quad(x_r, i)).then_inc(first_in[i], 16)
                if i < 2:
                    sp.dma_start(adj_i[:, i, :], tile(adj_r, 0, i)).then_inc(adj_in[i], 16)
            sp.dma_start(x_ln[:, :, :], quad(x_r, QB)).then_inc(xln_in, 16)
            sp.wait_ge(set_done, 1)
            sp.dma_start(table[ZERO_ROW:ZERO_ROW + 1, :], zeros).then_inc(zero_out, 16)
            sp.dma_start(w1_n, w1.rearrange("(k p) i -> p k i", p=P)).then_inc(w_in, 16)
            sp.dma_start(a_rows, a1).then_inc(w_in, 16)
            sp.dma_start(bias_row, bias1.rearrange("(a d) -> a d", a=1)).then_inc(w_in, 16)
            sp.dma_start(b0_row[:, :], b0.rearrange("(a d) -> a d", a=1)).then_inc(w_in, 16)
            sp.dma_start(w0_sb[:, :, :], w0.rearrange("(k p) o -> p k o", p=P)).then_inc(w_in, 16)
            sp.dma_start(table[N:2 * N, :], x_r[0:N, :]).then_inc(fill_out, 16)

            def store_table(q):
                sp.wait_ge(h_made, T * (q - QB) + T)
                sp.nop(nofuse=True)
                sp.dma_start(quad(table, q % TRING), h_ln[:, :, :]).then_inc(table_out, 16)

            def load_x_ln(q):
                sp.wait_ge(table_out, 16 * (q - QB))
                sp.nop(nofuse=True)
                sp.dma_start(x_ln[:, :, :], quad(x_r, q)).then_inc(xln_in, 16)

            def load_adj(q, t):
                if not (isinstance(q, int) and q == 0 and t < 2):
                    sp.wait_ge(nm_made, T * q + t - 1)
                    sp.nop(nofuse=True)
                sp.dma_start(adj_i[:, t % 2, :], tile(adj_r, q, t)).then_inc(adj_in[t % 2], 16)

            load_adj(0, 2)
            load_adj(0, 3)
            for i in range(QB):
                sp.wait_ge(first_made, (i + 1) * T)
                sp.dma_start(quad(table, i), h_first[:, i * T:(i + 1) * T, :]).then_inc(first_out, 16)
            load_adj(1, 0)
            load_adj(1, 1)
            sp.wait_ge(first_out, 16 * QB)
            sp.wait_ge(fill_out, 16)
            store_table(QB)
            sp.wait_ge(nm_out[0], 32)
            sp.wait_ge(nm_out[1], 32)
            sp.dma_start(nm_q[:, :, :], quad(nmask, 0)).then_inc(nm_in, 16)

            def step(s, lo, stages):
                a = s - LAG
                if "gather" in stages:
                    if lo > 0:
                        sp.wait_ge(x1_made, T * s)
                        sp.nop(nofuse=True)
                    sp.dma_start(h_q[:, :, :], quad(table, s % TRING)).then_inc(h_in, 16)
                    sp.dma_start(x_q[:, :, :], quad(x_r, s)).then_inc(x_in, 16)
                if "attend" in stages:
                    sp.dma_start(o_q[:, :, :], quad(xmid, a)).then_inc(x1_in, 16)
                if "index" in stages:
                    load_adj(s + 1, 2)
                    load_adj(s + 1, 3)
                if "table_rows" in stages:
                    store_table(s - 1 + AHEAD)
                if "table" in stages:
                    load_x_ln(s + AHEAD)
                if "load_index" in stages:
                    load_adj(s + 2, 0)
                    load_adj(s + 2, 1)
                if "attend" in stages:
                    sp.wait_ge(pen_made, NJ * (a + 1))
                    sp.nop(nofuse=True)
                    for u in range(2):
                        sp.wait_ge(nm_out[u], 16 * 2 * (a + 2))
                        sp.nop(nofuse=True)
                    sp.dma_start(nm_q[:, :, :], quad(nmask, a + 1)).then_inc(nm_in, 16)
                if "attend" in stages:
                    sp.wait_ge(out_made, a + 2)
                    sp.nop(nofuse=True)
                    sp.dma_start(quad(out_r, a), o_q[:, :, :]).then_inc(out_out, 16)
                if "gather" in stages:
                    sp.wait_ge(x1_made, T * s + T)
                    sp.nop(nofuse=True)
                    sp.dma_start(quad(xmid, s), x1_q[:, :, :]).then_inc(x1_out, 16)
                if "attend" in stages:
                    sp.wait_ge(out_out, 16 * (a + 1))
                    sp.nop(nofuse=True)
                if "gather" in stages:
                    sp.wait_ge(x1_out, 16 * (s + 1))
                    sp.nop(nofuse=True)

            schedule(sp, step)

            def attended(a):
                n = LAST - 4 + FINISHED.index(a)
                sp.wait_ge(out_made, n + 2)
                sp.dma_start(quad(out_r, a), o_q[:, :, :]).then_inc(out_out, 16)
                sp.wait_ge(out_out, 16 * (n + 1))

            sp.wait_ge(x1_made, T * LAST)
            sp.dma_start(h_q[:, :, :], quad(table, LAST % TRING)).then_inc(h_in, 16)
            sp.dma_start(x_q[:, :, :], quad(x_r, LAST)).then_inc(x_in, 16)
            sp.dma_start(o_q[:, :, :], quad(xmid, LAST - 4)).then_inc(x1_in, 16)
            sp.wait_ge(nm_made, T * QUADS)
            for u in range(2):
                sp.wait_ge(nm_out[u], 16 * 2 * QUADS)
            sp.dma_start(nm_adj, quad(nmask, LAST - 3)).then_inc(nm_adj_in, 16)
            sp.wait_ge(pen_made, NJ * (LAST - 3))
            sp.dma_start(nm_q[:, :, :], quad(nmask, LAST - 2)).then_inc(nm_in, 16)
            attended(LAST - 4)
            sp.wait_ge(agg_made, T * QUADS + 2)
            sp.dma_start(nm_near, nmask[(LAST - 1) * QR:QUADS * QR, :].rearrange("(t p) n -> p t n", p=P)
                         ).then_inc(nm_near_in, 16)
            sp.wait_ge(x1_made, T * QUADS)
            sp.dma_start(quad(xmid, LAST), x1_q[:, :, :]).then_inc(x1_out, 16)
            sp.wait_ge(x1_out, 16 * QUADS)
            for a in FINISHED[1:]:
                sp.dma_start(o_q[:, :, :], quad(xmid, a)).then_inc(x1_in, 16)
                attended(a)
            sp.wait_ge(zero_out, 16)
            sp.wait_ge(table_out, 16 * (QUADS - QB))
            sp.wait_ge(nm_out[0], 16 * 2 * QUADS)
            sp.wait_ge(nm_out[1], 16 * 2 * QUADS)
            sp.wait_ge(x1_out, 16 * QUADS)
            sp.wait_ge(out_out, 16 * QUADS)

        @block.gpsimd
        def _(pool):
            pool.wait_ge(zero_out, 16)
            pool.wait_ge(first_out, 16 * QB)
            pool.wait_ge(fill_out, 16)

            def step(s, lo, stages):
                if "gather" not in stages:
                    return
                if lo > 0:
                    pool.wait_ge(table_out, 16 * s if "table_rows" in stages else 16 * (QUADS - QB))
                for t in range(T):
                    if t % 2 == 0:
                        pool.wait_ge(idx_ready, 2 * s + t // 2 + 1)
                    pool.wait_ge(agg_made, T * s + t + 1)
                    pool.nop(nofuse=True)
                    for k in range(S):
                        pool.indirect_dma_start(
                            out=near[:, t % 2, k, :], out_offset=None, in_=table,
                            in_offset=bass.IndirectOffsetOnAxis(ap=idx[:, t, k:k + 1], axis=0),
                        ).then_inc(near_in[t % 2], 16)

            schedule(pool, step)
            step(LAST, LAST, {"gather"})

        @block.scalar
        def _(act):
            b1 = bank1_uses()
            act.wait_ge(cst_in, 16)
            nc.scalar.activation(ident_b[:, :], ident, ACT.Copy)
            nc.scalar.activation(neg_ident[:, :], ident, ACT.Copy, scale=-1.0)
            nc.scalar.activation(pack_w[:, :], cst[:, C_PK:C_PK + P // GB], ACT.Copy).then_inc(set_act, 1)

            def setup_weights():
                act.wait_ge(set_pe, 1)
                nc.scalar.activation(w1_t[:, :, 0:C], bank1[:, :].rearrange("p (k c) -> p k c", k=KC),
                                     ACT.Copy).then_inc(set_act, 1)
                act.wait_ge(set_pe, 2)
                nc.scalar.activation(a_t[:, :, :], bank1[:, 0:2 * KC].rearrange("p (k c) -> p k c", k=KC),
                                     ACT.Copy).then_inc(set_act, 1)
                act.wait_ge(set_pe, 3)
                nc.scalar.activation(w1_t[:, :, C:C + 2], bank1[:, 0:2 * KC].rearrange("p (k c) -> p k c", k=KC),
                                     ACT.Copy).then_inc(set_act, 1)
                act.wait_ge(set_pe, 4)
                nc.scalar.activation(bias_b[:, :], bank1[:, 0:C], ACT.Copy)
                act.wait_ge(set_act, 4)
                act.wait_ge(set_done, 2)
                for k in range(KC):
                    ins = nc.scalar.activation(wa2_b[:, k, :], ones_f[:, :], ACT.Copy,
                                               scale=w1_t[:, k, C + 1:C + 2])
                ins.then_inc(set_act, 1)

            def index_masks(q, pair, first):
                for u in range(2):
                    t = 2 * pair + u
                    act.wait_ge(adj_in[u], 16 * (2 * q + pair + 1))
                    if not (first and pair == 0):
                        act.wait_ge(nm_out[u], 16 * (2 * q + pair))
                    nc.scalar.activation(nm_t[:, u, :], adj_i[:, u, :], ACT.Relu, bias=BIG_B, scale=-BIG
                                         ).then_inc(nm_made, 1)
                for u in range(2):
                    t = 2 * pair + u
                    act.wait_ge(nm_made, T * q + t + 1)
                    act.dma_start(tile(nmask, q, t), nm_t[:, u, :]).then_inc(nm_out[u], 16)

            def index_half(q, pair, half, first):
                h = 4 * pair + half
                act.wait_ge(b1_full, b1.next())
                if not (first and h < 2):
                    act.wait_ge(packed, 2 * T * q + h - 1)
                nc.scalar.activation(nm_x[:, half % 2, :], bank1_b[:, :], ACT.Copy).then_inc(nmx_made, 1)
                act.wait_ge(nmx_made, 2 * T * q + h + 1)
                act.sem_inc(b1_free, 1)

            def normalise(q, first_col, src, dst, ready, made):
                act.wait_ge(ready, q + 1)
                for t in range(T):
                    c = first_col + t
                    nc.scalar.activation(dst[:, t, :], src[:, t, :], ACT.Relu, bias=shift[:, c:c + 1],
                                         scale=rstd[:, c:c + 1]).then_inc(made, 1)

            def project(q, normalised=h2_q, between=lambda: None):
                normalise(q, T, x1_q, normalised, ln2_ready, h2_made)
                act.wait_ge(proj_pe, 2 * q + 1)
                nc.scalar.activation(h2_t[:, :, :], acc[:, 0:KC, :], ACT.Copy).then_inc(h2t_made, 1)
                between()
                act.wait_ge(b1_full, b1.next())
                nc.scalar.activation(a2_all[:, bass.ds((q % RING) * QR, QR)], bank1[:, :], ACT.Copy
                                     ).then_inc(b1_free, 1)

            def hidden(q):
                act.wait_ge(proj_pe, 2 * q + 2)
                nc.scalar.activation(hid[:, bass.ds((q % RING) * T, T), 1:C + 3], acc[:, :, 0:C + 2], ACT.Copy
                                     ).then_inc(hid_made, 1)

            def leaky(g, c, row):
                for i in range(2):
                    j = 2 * c + i
                    act.wait_ge(arg_made, 2 * g + i + 1)
                    nc.scalar.activation(lin[:, i, :], row, ACT.Relu, bias=a2_rise[:, j:j + 1],
                                         scale=RISE).then_inc(lin_made, 1)

            def weights(g, half):
                act.wait_ge(arg_made, 2 * g + 4)
                nc.scalar.activation(wgt[:, half, :], wgt[:, half, :], ACT.Exp).then_inc(wgt_made, 1)

            def chunk(a, c):
                if c + 1 < NJ // 2:
                    leaky(NJ // 2 * a + c + 1, c + 1, a1_b[:, :])
                weights(NJ // 2 * a + c, c % 2)

            def row_scores(to):
                act.wait_ge(b1_full, b1.next())
                nc.scalar.activation(to, bank1[:, :], ACT.Copy).then_inc(b1_free, 1)

            def row_maxima(to):
                act.wait_ge(b1_full, b1.next())
                nc.scalar.activation(to, bank1_b[0:3, 0:QR], ACT.Copy).then_inc(b1_free, 1)

            def task_setup(k):
                row_scores(a1_rows[k % 3])
                row_maxima(m_rows[k % 3])

            def task_starts(k):
                act.wait_ge(b1_free, b1.n + 1)
                if k == 1:
                    act.wait_ge(cols_made, 1)
                leaky(TASK_AT[k], TASKS[k][1], a1_rows[k % 3])

            def rescaling(i):
                act.wait_ge(dist_made, i + 1)
                nc.scalar.activation(scale_p[:, i, :], scale_p[:, i, :], ACT.Exp).then_inc(scale_made, 1)

            def last_quad():
                project(LAST - 1)
                hidden(LAST - 1)
                act.wait_ge(packed, 2 * T * QUADS)
                task_setup(0)
                cat_copy()
                task_starts(0)
                for k in range(len(TASKS)):
                    a, first, count = TASKS[k]
                    for c in range(count):
                        if c + 1 < count:
                            leaky(TASK_AT[k] + c + 1, first + c + 1, a1_rows[k % 3])
                        elif k + 1 < len(TASKS) and k != 1:
                            task_starts(k + 1)
                        weights(TASK_AT[k] + c, c % 2)
                        for n, at in (1, (0, 5)), (3, (2, 3)), (5, (4, 4)):
                            if (k, c) == at:
                                row_scores(a1_rows[n % 3])
                        for n, at in (1, (0, 6)), (3, (2, 4)), (5, (4, 5)):
                            if (k, c) == at:
                                row_maxima(m_rows[n % 3])
                        if (k, c) in ((2, 4), (4, 5)):
                            rescaling(k // 2 - 1)
                        if (k, c) == (3, 0):
                            task_setup(4)
                        if (k, c) == (5, 0):
                            task_setup(6)
                        if (k, c) in ((0, 1), (0, 6), (1, 2)):
                            cat_copy()
                    if k == 1:
                        project(LAST, x_q, lambda: task_setup(2))
                        act.wait_ge(b1_free, b1.n + 1)
                        act.sem_inc(a2_made, 1)
                        task_starts(2)
                        hidden(LAST)

            def cat_copy():
                act.wait_ge(b1_full, b1.next())
                nc.scalar.activation(cat_t, bank1[:, :], ACT.Copy).then_inc(b1_free, 1)

            def step(s, lo, stages):
                b1.start(s, lo)
                a = s - LAG

                def attended(c, half=None):
                    if "attend" in stages:
                        chunk(a, c)
                    if "index" in stages and half is not None:
                        index_half(s + 1, 1, half, False)

                def gathered():
                    if "gather" in stages:
                        cat_copy()

                if "index" in stages:
                    index_masks(s + 1, 0, False)
                    for half in range(4):
                        index_half(s + 1, 0, half, False)
                if "project" in stages:
                    project(s - 1)
                if "attend" in stages:
                    act.wait_ge(b1_free, b1.n + 1)
                    act.wait_ge(out_made, a + 1)
                    nc.scalar.activation(a2_row, a2_all[:, bass.ds((a % RING) // QB * N, N)], ACT.Copy
                                         ).then_inc(a2_made, 1)
                if "project" in stages:
                    hidden(s - 1)
                if "table_rows" in stages:
                    normalise(s, 0, x_ln, h_ln, ln1_ready, h_made)
                gathered()
                if "index" in stages:
                    index_masks(s + 1, 1, False)
                if "attend" in stages:
                    row_scores(a1_b[:, :])
                    row_maxima(m_r[:, :])
                    act.wait_ge(b1_free, b1.n + 1)
                    leaky(NJ // 2 * a, 0, a1_b[:, :])
                gathered()
                for c in range(4):
                    attended(c, c)
                gathered()
                for c in range(4, 8):
                    attended(c)
                gathered()

            act.sem_inc(b1_free, 1)
            act.wait_ge(set_done, 3)
            BIG_B = big_c[:, :]
            b1.start(-1, -1)
            index_masks(0, 0, True)
            for half in range(4):
                index_half(0, 0, half, True)
            act.wait_ge(first_ready, 1)
            for t in range(NJ):
                nc.scalar.activation(h_first[:, t, :], x_first[:, t, :], ACT.Relu, bias=shift[:, t:t + 1],
                                     scale=rstd[:, t:t + 1]).then_inc(first_made, 1)
            index_masks(0, 1, True)
            for half in range(4):
                index_half(0, 1, half, True)
            normalise(0, 0, x_ln, h_ln, ln1_ready, h_made)
            setup_weights()
            schedule(act, step)
            b1.start(LAST, LAST)
            last_quad()

        @block.vector
        def _(dve):
            b2 = bank2_uses()

            nc.vector.memset(agg[:, :], 0.0).then_inc(set_done, 1)
            nc.vector.memset(ones_f[:, :], 1.0).then_inc(set_done, 1)
            nc.vector.memset(big_c[:, :], BIG).then_inc(set_done, 1)
            nc.vector.memset(ones_b[:, :], 1.0)
            nc.vector.memset(hid[:, :, 0:1], 1.0)
            dve.wait_ge(cst_in, 16)
            nc.vector.tensor_copy(pow_i[:, :], cst[:, C_POW:C_POW + GB]).then_inc(set_done, 1)
            dve.wait_ge(set_done, 4)
            dve.sem_inc(agg_made, 2)
            dve.sem_inc(b2_free, 1)
            dve.sem_inc(arg_made, 2)
            dve.sem_inc(out_made, 1)

            def statistics(cols, sources, ready, arrived=lambda c: None):
                lo, hi = cols
                chain, cnt = ln_step, Count()
                for c, src in sources:
                    arrived(c)
                    ins = nc.vector.bn_stats(stat[:, c, :], src)
                ins.then_inc(chain, 1)
                dve.wait_ge(chain, cnt.next())
                for c, _ in sources:
                    ins = nc.vector.bn_aggr(mv[:, c, :], stat[:, c, :])
                ins.then_inc(chain, 1)
                dve.wait_ge(chain, cnt.next())
                v, y, n = var[:, lo:hi], rstd[:, lo:hi], nwt[:, lo:hi]
                nc.vector.tensor_scalar(v, mv[:, lo:hi, 1], EPS, None, ALU.add).then_inc(chain, 1)
                dve.wait_ge(chain, cnt.next())
                nc.vector.tensor_scalar(rsq_i[:, lo:hi], v.bitcast(I32), 1, None, ALU.arith_shift_right
                                        ).then_inc(chain, 1)
                dve.wait_ge(chain, cnt.next())
                nc.vector.tensor_scalar(y.bitcast(I32), rsq_i[:, lo:hi], -1.0, float(0x5F3759DF), ALU.mult, ALU.add
                                        ).then_inc(chain, 1)
                dve.wait_ge(chain, cnt.next())
                for _ in range(3):
                    nc.vector.tensor_tensor(n, y, y, ALU.mult).then_inc(chain, 1)
                    dve.wait_ge(chain, cnt.next())
                    nc.vector.scalar_tensor_tensor(n, n, -0.5, v, ALU.mult, ALU.mult).then_inc(chain, 1)
                    dve.wait_ge(chain, cnt.next())
                    nc.vector.scalar_tensor_tensor(y, n, 1.5, y, ALU.add, ALU.mult).then_inc(chain, 1)
                    dve.wait_ge(chain, cnt.next())
                nc.vector.scalar_tensor_tensor(shift[:, lo:hi], mv[:, lo:hi, 0], -1.0, y, ALU.mult, ALU.mult
                                               ).then_inc(ready, 1)
                dve.sem_clear(chain)

            def table_alone():
                dve.wait_ge(xln_in, 16)
                dve.wait_ge(first_made, NJ)
                statistics((0, T), [(t, x_ln[:, t, :]) for t in range(T)], ln1_ready)

            def statistics_of_step(s, stages):
                dve.wait_ge(x1_made, T * s + T)
                if "table" in stages:
                    dve.wait_ge(xln_in, 16 * (s + 2))
                    cols, src = (0, 2 * T), [(t, x_ln[:, t, :]) for t in range(T)]
                else:
                    cols, src = (T, 2 * T), []
                src = src + [(T + t, x1_q[:, t, :]) for t in range(T)]
                statistics(cols, src, ln2_ready)
                if "table" in stages:
                    dve.wait_ge(ln2_ready, s + 1)
                    dve.sem_inc(ln1_ready, 1)

            def top_rounds(src, ix_n):
                for r in range(TOP // 8):
                    seen = []
                    for u in range(2):
                        if r > 0:
                            dve.wait_ge(ix_step, gone[u])
                        nc.vector.max(top[:, u, 8 * r:8 * r + 8], src[:, u, :]).then_inc(ix_step, 1)
                        seen.append(ix_n.next())
                    gone = []
                    if r < TOP // 8 - 1:
                        for u in range(2):
                            dve.wait_ge(ix_step, seen[u])
                            nc.vector.match_replace(src[:, u, :], top[:, u, 8 * r:8 * r + 8], src[:, u, :], PADKEY
                                                    ).then_inc(ix_step, 1)
                            gone.append(ix_n.next())
                dve.wait_ge(ix_step, seen[1])

            def index_words(q):
                words = bank2[:, :].rearrange("p (u g) -> p u g", u=2)
                dve.wait_ge(b2_full, b2.next())
                base = word_base.unsqueeze(1).to_broadcast([P, 2, NG])
                nc.vector.scalar_tensor_tensor(key2[:, :, :], words, -(2.0 ** GB - 1.5), base, ALU.is_gt, ALU.mult
                                               ).then_inc(ix_step, 1)
                dve.wait_ge(ix_step, 1)
                nc.vector.tensor_tensor(key[:, :, :], key2[:, :, :], words, ALU.add).then_inc(b2_free, 1)
                nc.vector.tensor_copy(code[:, :], cst[:, bass.ds(q * 2 + C_CODE, 2)]).then_inc(ix_step, 1)

            def index_rest(q, pair, between):
                ix_n = Count(2)
                dve.wait_ge(ix_step, 2)
                top_rounds(key, ix_n)
                nc.vector.tensor_scalar(top_i[:, :], top[:, :, :].rearrange("p u k -> p (u k)"), 0.0, None, ALU.max
                                        ).then_inc(ix_step, 1)
                dve.wait_ge(ix_step, ix_n.next())
                words_i = top_i[:, :].unsqueeze(2).to_broadcast([P, 2 * TOP, GB])
                powers = pow_i[:, :].unsqueeze(1).to_broadcast([P, 2 * TOP, GB])
                nc.vector.tensor_tensor(bits[:, :].rearrange("p (k j) -> p k j", j=GB), words_i, powers,
                                        ALU.bitwise_and).then_inc(ix_step, 1)
                ix_n.next()
                nc.vector.tensor_scalar(high_i[:, :], top_i[:, :], (2 ** GB - 1) ^ 0xFFFFF, None, ALU.bitwise_and
                                        ).then_inc(ix_step, 1)
                dve.wait_ge(ix_step, ix_n.next())
                high = high_i[:, :].unsqueeze(2).to_broadcast([P, 2 * TOP, GB])
                place = cst[:, C_J:C_J + GB].unsqueeze(1).to_broadcast([P, 2 * TOP, GB])
                nc.vector.scalar_tensor_tensor(
                    key2[:, :, :].rearrange("p u (k j) -> p (u k) j", j=GB), high, GB / 2.0 ** GB, place,
                    ALU.mult, ALU.subtract).then_inc(ix_step, 1)
                dve.wait_ge(ix_step, ix_n.next())
                nc.vector.scalar_tensor_tensor(
                    key[:, :, :].rearrange("p u g -> p (u g)"), bits[:, :], 0.0,
                    key2[:, :, :].rearrange("p u g -> p (u g)"), ALU.is_gt, ALU.mult).then_inc(ix_step, 1)
                between()
                dve.wait_ge(ix_step, ix_n.next())
                top_rounds(key, ix_n)
                nc.vector.tensor_scalar(miss[:, :, :], top[:, :, :], 0.0, code[:, 1:2], ALU.is_equal, ALU.mult
                                        ).then_inc(ix_step, 1)
                dve.wait_ge(ix_step, ix_n.next())
                nc.vector.scalar_tensor_tensor(idx[:, 2 * pair:2 * pair + 2, :], miss[:, :, :], code[:, 0:1],
                                               top[:, :, :], ALU.add, ALU.subtract).then_inc(idx_ready, 1)
                dve.sem_clear(ix_step)

            def maximum(s, t):
                dve.wait_ge(near_in[t % 2], 16 * S * (2 * s + t // 2 + 1))
                nc.vector.tensor_reduce(agg[:, :], near[:, t % 2, :, :].rearrange("p k c -> p c k"), AX.X, ALU.max
                                        ).then_inc(agg_made, 1)

            def residual0(s, t, lo):
                if t == 0:
                    dve.wait_ge(x_in, 16 * (s + 1))
                    dve.wait_ge(h_in, 16 * (s + 1))
                    if lo > 0:
                        dve.wait_ge(h2_made, T * s)
                dve.wait_ge(b2_full, b2.next())
                nc.vector.scalar_tensor_tensor(x1_q[:, t, :], bank2[:, 0:C], 0.0, x_q[:, t, :], ALU.max, ALU.add
                                               ).then_inc(b2_free, 1)
                dve.wait_ge(b2_free, b2.n + 1)
                dve.sem_inc(x1_made, 1)

            def largest(scores, non_edges, scratch, tiles, as_n, to=amax):
                for t in tiles:
                    nc.vector.tensor_tensor_reduce(
                        out=scratch, in0=scores, in1=non_edges[:, t, :], scale=1.0,
                        scalar=-3.0e38, op0=ALU.subtract, op1=ALU.max, accum_out=to[:, t:t + 1]
                        ).then_inc(as_step, 1)
                    dve.wait_ge(as_step, as_n.next())

            def column_scores(a, lo=0, hi=NJ):
                batch = (a % RING) // QB
                scores = hid[:, bass.ds(batch * NJ + lo, hi - lo), C + 2]
                nc.vector.tensor_scalar(a2_slope[:, lo:hi], scores, SLOPE, None, ALU.mult)
                return nc.vector.tensor_scalar(a2_rise[:, lo:hi], scores, RISE, None, ALU.mult)

            def attend_setup(a, lo):
                as_n = Count()
                dve.wait_ge(nm_in, 16 * (a + 1))
                dve.wait_ge(a2_made, a + 1)
                dve.nop(nofuse=True)
                largest(a2_row, nm_q, junk, range(T), as_n)
                dve.wait_ge(hid_made, a + LAG)
                column_scores(a)
                row_setup(a, diag, as_n, lambda: None)

            def row_setup(a, diagonals, as_n, between, amax=amax[:, :], nmax=nmax[:, :]):
                nc.vector.tensor_copy(a1_c[:, :], hid[:, bass.ds((a % RING) * T, T), C + 1]).then_inc(as_step, 1)
                as_n.next()
                nc.vector.tensor_scalar(lone[:, :], amax, -BIG / 2, None, ALU.is_lt).then_inc(as_step, 1)
                lone_n = as_n.next()
                nc.vector.scalar_tensor_tensor(cmax[:, :], amax, -BIG / 2, amax, ALU.is_ge, ALU.mult
                                               ).then_inc(as_step, 1)
                as_n.next()
                dve.wait_ge(as_step, lone_n)
                nc.vector.scalar_tensor_tensor(a1_p[:, :], lone[:, :], FAR, a1_c[:, :], ALU.mult, ALU.add
                                               ).then_inc(as_step, 1)
                dve.wait_ge(as_step, as_n.next())
                nc.vector.tensor_tensor(diagonals, ident.unsqueeze(1).to_broadcast([P, T, P]),
                                        a1_p[:, :].unsqueeze(2).to_broadcast([P, T, P]), ALU.mult
                                        ).then_inc(diag_made, 1)
                nc.vector.tensor_tensor(rest[:, :], a1_c[:, :], cmax[:, :], ALU.add).then_inc(as_step, 1)
                between()
                dve.wait_ge(as_step, as_n.next())
                nc.vector.scalar_tensor_tensor(rmax[:, :], rest[:, :], SLOPE, rest[:, :], ALU.mult, ALU.max
                                               ).then_inc(as_step, 1)
                dve.wait_ge(as_step, as_n.next())
                nc.vector.scalar_tensor_tensor(rest[:, :], a1_c[:, :], SLOPE, rmax[:, :], ALU.mult, ALU.subtract
                                               ).then_inc(as_step, 1)
                dve.wait_ge(as_step, as_n.next())
                nc.vector.scalar_tensor_tensor(nmax, lone[:, :], LONE, rest[:, :], ALU.mult, ALU.add
                                               ).then_inc(as_step, 1)
                dve.wait_ge(as_step, as_n.next())
                nc.vector.tensor_copy(m_c[:, :, 0], nmax).then_inc(as_step, 1)
                dve.wait_ge(as_step, as_n.next())
                nc.vector.tensor_tensor(rest[:, :], nmax, m_c[:, :, 0], ALU.subtract).then_inc(as_step, 1)
                dve.wait_ge(as_step, as_n.next())
                nc.vector.tensor_copy(m_c[:, :, 1], rest[:, :]).then_inc(as_step, 1)
                dve.wait_ge(as_step, as_n.next())
                nc.vector.tensor_tensor(m_c[:, :, 2], rest[:, :], m_c[:, :, 1], ALU.subtract).then_inc(m_made, 1)
                dve.sem_clear(as_step)

            def exponents(g, c):
                dve.wait_ge(wgt_used, g + 1)
                for i in range(2):
                    j = 2 * c + i
                    dve.wait_ge(pen_made, 2 * g + i + 1)
                    dve.wait_ge(lin_made, 2 * g + i + 1)
                    nc.vector.scalar_tensor_tensor(wgt[:, c % 2, i * QR:(i + 1) * QR], pen[:, i, :],
                                                   a2_slope[:, j:j + 1], lin[:, i, :], ALU.add, ALU.add
                                                   ).then_inc(arg_made, 1)

            def chunk(a, c):
                exponents(NJ // 2 * a + c, c)

            def attend_end(a, scaled, k=None):
                af_n = Count()
                g = NJ // 2 * (a + 1) if k is None else TASK_AT[k] + TASKS[k][2]
                n = a if k is None else LAST - 4 + FINISHED.index(a)
                dve.wait_ge(wgt_used, g + 2)
                dve.wait_ge(x1_in, 16 * (n + 1))
                nc.vector.reciprocal(rden[:, :], acc[:, :, 0]).then_inc(af_step, 1)
                dve.wait_ge(af_step, af_n.next())
                for t in range(T):
                    ins = nc.vector.scalar_tensor_tensor(scaled[:, t, :], acc[:, t, 1:C + 1], rden[:, t:t + 1],
                                                         bias_b[:, :], ALU.mult, ALU.add)
                if k is not None:
                    ins.then_inc(acc_read, 1)
                    dve.wait_ge(acc_read, k + 1)
                else:
                    ins.then_inc(af_step, 1)
                    dve.wait_ge(af_step, af_n.next())
                nc.vector.tensor_tensor(o_q[:, :, :], scaled[:, :, :], o_q[:, :, :], ALU.add).then_inc(out_made, 1)
                dve.sem_clear(af_step)

            def keep_part(k):
                i = TASKS[k][0] - (LAST - 3)
                dve.wait_ge(wgt_used, TASK_AT[k] + TASKS[k][2] + 2)
                nc.vector.tensor_copy(sum_p[:, i, :], acc[:, :, 0])
                nc.vector.tensor_copy(part[TASKS[k][0]][:, :, :], acc[:, :, 1:C + 1]).then_inc(acc_read, 1)

            def join_parts(k):
                af_n = Count()
                a = TASKS[k][0]
                i = a - (LAST - 3)
                sums = part[a]
                dve.wait_ge(wgt_used, TASK_AT[k] + TASKS[k][2] + 2)
                dve.wait_ge(scale_made, i + 1)
                dve.wait_ge(x1_in, 16 * (LAST - 3 + FINISHED.index(a)))
                nc.vector.tensor_tensor(sum_p[:, i, :], sum_p[:, i, :], scale_p[:, i, :], ALU.mult
                                        ).then_inc(af_step, 1)
                dve.wait_ge(af_step, af_n.next())
                nc.vector.tensor_tensor(sum_p[:, i, :], sum_p[:, i, :], acc[:, :, 0], ALU.add).then_inc(af_step, 1)
                sums_n = af_n.next()
                for t in range(T):
                    ins = nc.vector.scalar_tensor_tensor(sums[:, t, :], sums[:, t, :], scale_p[:, i, t:t + 1],
                                                         acc[:, t, 1:C + 1], ALU.mult, ALU.add)
                ins.then_inc(acc_read, 1)
                dve.wait_ge(af_step, sums_n)
                nc.vector.reciprocal(rden[:, :], sum_p[:, i, :]).then_inc(af_step, 1)
                dve.wait_ge(af_step, af_n.next())
                dve.wait_ge(acc_read, k + 1)
                for t in range(T):
                    ins = nc.vector.scalar_tensor_tensor(sums[:, t, :], sums[:, t, :], rden[:, t:t + 1],
                                                         bias_b[:, :], ALU.mult, ALU.add)
                ins.then_inc(af_step, 1)
                dve.wait_ge(af_step, af_n.next())
                nc.vector.tensor_tensor(o_q[:, :, :], sums[:, :, :], o_q[:, :, :], ALU.add).then_inc(out_made, 1)
                dve.sem_clear(af_step)

            def last_quad():
                n0 = KNOWN * 2 * P
                first = LAST - 3
                diagonals = diag_last.rearrange("p (t c) -> p t c", t=T)

                def largest_known(a, tiles, as_n):
                    largest(a2_of(a)[:, 0:n0], nm_of[a][:, :, 0:n0], junk_last[:, 0:n0], tiles, as_n,
                            amax_q[:, a - first, :])

                def largest_whole(a, tiles, as_n):
                    largest(a2_of(a), nm_of[a], junk_last, tiles, as_n, amax_q[:, a - first, :])

                def largest_all(a, as_n):
                    largest(a2_of(a)[:, n0:N], nm_of[a][:, :, n0:N], junk_last[:, n0:N], range(T), as_n, rest)
                    so_far = amax_q[:, a - first, :]
                    nc.vector.tensor_tensor(so_far, so_far, rest[:, :], ALU.max).then_inc(as_step, 1)
                    dve.wait_ge(as_step, as_n.next())

                def setup(k, as_n, between=lambda: None, nmax=nmax[:, :]):
                    a = TASKS[k][0]
                    row_setup(a, diagonals, as_n, between, amax_q[:, a - first, :], nmax)

                def distance(i):
                    dist = scale_p[:, i, :]
                    nc.vector.tensor_tensor(dist, nmax[:, :], nmax_p[:, i, :], ALU.subtract).then_inc(af_step, 1)
                    dve.wait_ge(af_step, 1)
                    nc.vector.scalar_tensor_tensor(dist, dist, -1.0, dist, ALU.mult, ALU.min).then_inc(dist_made, 1)
                    dve.sem_clear(af_step)

                def task(k, *chunks):
                    for c in chunks:
                        exponents(TASK_AT[k] + c, TASKS[k][1] + c)

                for u in range(2):
                    dve.wait_ge(nm_out[u], 16 * 2 * QUADS)
                dve.wait_ge(packed, 2 * T * QUADS)
                dve.wait_ge(table_out, 16 * (QUADS - QB))
                as_n = Count()
                dve.wait_ge(nm_in, 16 * (LAST - 3))
                dve.wait_ge(hid_made, LAST - 3)
                largest(a2_of(LAST - 4), nm_of[LAST - 4], junk_last, range(T), as_n)
                column_scores(LAST - 4)
                row_setup(LAST - 4, diagonals, as_n, lambda: None)
                maximum(LAST, 0)

                def meanwhile():
                    task(0, 0)
                    residual0(LAST, 0, LAST)

                index_rest(LAST, 1, meanwhile)
                task(0, 1)
                maximum(LAST, 1)
                as_n = Count()
                dve.wait_ge(hid_made, LAST)
                dve.wait_ge(nm_adj_in, 16)
                largest_known(first, (0, 1), as_n)
                task(0, 2)
                largest_known(first, (2, 3), as_n)
                residual0(LAST, 1, LAST)
                task(0, 3)
                setup(1, as_n, lambda: task(0, 4), nmax_p[:, 0, :])
                task(0, 5, 6)
                maximum(LAST, 2)
                task(0, 7)
                column_scores(first, 0, 2 * KNOWN).then_inc(cols_made, 1)
                residual0(LAST, 2, LAST)
                task(1, 0)
                attend_end(LAST - 4, h_ln, 0)
                task(1, 1)
                as_n = Count()
                dve.wait_ge(nm_in, 16 * (LAST - 2))
                largest_known(first + 1, (0, 1), as_n)
                task(1, 2)
                maximum(LAST, 3)
                task(1, 3, 4)
                residual0(LAST, 3, LAST)
                statistics_of_step(LAST, ())
                task(1, 5)
                largest_known(first + 1, (2, 3), as_n)
                keep_part(1)
                setup(2, as_n, nmax=nmax_p[:, 1, :])
                task(2, 0)
                as_n = Count()
                dve.wait_ge(a2_made, LAST - 3)
                largest_all(first, as_n)
                task(2, 1)
                dve.wait_ge(hid_made, QUADS)
                column_scores(first, 2 * KNOWN, NJ)
                setup(3, as_n, lambda: task(2, 2))
                distance(0)
                task(2, 3)
                as_n = Count()
                dve.wait_ge(nm_near_in, 16)
                largest_whole(LAST - 1, (0, 1), as_n)
                task(2, 4)
                largest_whole(LAST - 1, (2, 3), as_n)
                task(2, 5)
                task(3, 0)
                setup(4, as_n)
                keep_part(2)
                task(3, 1)
                task(4, 0)
                join_parts(3)
                task(4, 1)
                as_n = Count()
                largest_all(first + 1, as_n)
                task(4, 2)
                setup(5, as_n, lambda: task(4, 3))
                distance(1)
                as_n = Count()
                task(4, 4)
                largest_whole(LAST, (0, 1), as_n)
                task(4, 5)
                largest_whole(LAST, (2, 3), as_n)
                task(4, 6)
                setup(6, as_n)
                task(4, 7)
                task(5, 0)
                attend_end(LAST - 1, x_ln, 4)
                task(5, 1)
                task(6, 0)
                join_parts(5)
                task(6, 1, 2, 3, 4, 5, 6, 7)
                attend_end(LAST, x_ln, 6)

            def step(s, lo, stages):
                b2.start(s, lo)
                a = s - LAG

                def attended(*chunks):
                    if "attend" in stages:
                        for c in chunks:
                            chunk(a, c)

                def gathered(t):
                    if "gather" in stages:
                        maximum(s, t)

                def finished(t):
                    if "gather" in stages:
                        residual0(s, t, lo)

                if "index" in stages:
                    index_words(s + 1)
                gathered(0)
                if "attend" in stages:
                    attend_setup(a, lo)
                finished(0)
                gathered(1)
                attended(0)
                if "index" in stages:
                    def between():
                        finished(1)
                        attended(1)
                    index_rest(s + 1, 0, between)
                else:
                    finished(1)
                    attended(1)
                attended(2, 3)
                gathered(2)
                if "index" in stages:
                    index_words(s + 1)
                attended(4)
                finished(2)
                attended(5, 6, 7)
                gathered(3)
                if "attend" in stages:
                    attend_end(a, near_out)
                finished(3)
                if "gather" in stages:
                    statistics_of_step(s, stages)
                if "index" in stages and lo < LAST - 1:
                    index_rest(s + 1, 1, lambda: None)

            near_out = wgt_flat[:, 0:T * C].rearrange("p (t c) -> p t c", t=T)
            b2.start(-1, -1)
            statistics((0, NJ), [(t, x_first[:, t, :]) for t in range(NJ)], first_ready,
                       lambda c: dve.wait_ge(first_in[c // T], 16))
            index_words(0)
            index_rest(0, 0, lambda: None)
            table_alone()
            index_words(0)
            index_rest(0, 1, lambda: None)
            dve.wait_ge(zero_out, 16)
            schedule(dve, step)
            b2.start(LAST, LAST)
            last_quad()

        @block.tensor
        def _(pe):
            b1, b2 = bank1_uses(), bank2_uses()

            def setup_weights():
                pe.wait_ge(w_in, 80)
                pe.wait_ge(cst_in, 16)
                for o in range(KC):
                    for i in range(KC):
                        mm = nc.tensor.transpose(bank1[:, i * C + o * P:i * C + (o + 1) * P],
                                                 w1_n[:, o, i * P:(i + 1) * P], ident)
                mm.then_inc(set_pe, 1)
                pe.wait_ge(set_act, 2)
                for o in range(KC):
                    mm = nc.tensor.transpose(bank1[:, 2 * o:2 * o + 2], a_rows[:, o * P:(o + 1) * P], ident[0:2, 0:2])
                mm.then_inc(set_pe, 1)
                pe.wait_ge(set_act, 3)
                for i in range(KC):
                    for o in range(KC):
                        mm = nc.tensor.matmul(bank1[:, 2 * i:2 * i + 2], w1_n[:, o, i * P:(i + 1) * P], a_t[:, o, :],
                                              start=(o == 0), stop=(o == KC - 1))
                mm.then_inc(set_pe, 1)
                pe.wait_ge(set_act, 4)
                pe.wait_ge(set_done, 2)
                nc.tensor.matmul(bank1[:, 0:C], ones_f[0:1, :], bias_row, start=True, stop=True
                                 ).then_inc(set_pe, 1)
                pe.wait_ge(set_act, 5)
                pe.wait_ge(set_done, 4)
                pe.sem_inc(wgt_used, 2)

            def index_transpose(q, pair, half):
                u = half // 2
                pe.wait_ge(nm_made, T * q + 2 * pair + u + 1)
                pe.wait_ge(b1_free, b1.next())
                for i in range(NJ // 2):
                    j = half % 2 * NJ // 2 + i
                    mm = nc.tensor.transpose(bank1_b[:, i * P:(i + 1) * P], nm_t[:, u, j * P:(j + 1) * P],
                                             ident_b[:, :])
                mm.then_inc(b1_full, 1)

            def index_pack(q, pair, half):
                u = half // 2
                if half == 0:
                    pe.wait_ge(b2_free, b2.next())
                pe.wait_ge(nmx_made, 2 * T * q + 4 * pair + half + 1)
                for i in range(NJ // 2):
                    j = half % 2 * NJ // 2 + i
                    w = P // GB
                    mm = nc.tensor.matmul(bank2[:, u * NG + j * w:u * NG + (j + 1) * w],
                                          nm_x[:, half % 2, i * P:(i + 1) * P], pack_w[:, :],
                                          start=True, stop=True)
                mm.then_inc(packed, 1)
                if half == 3:
                    pe.wait_ge(packed, 2 * T * q + 4 * pair + 4)
                    pe.sem_inc(b2_full, 1)

            def index_prep(q, pair):
                index_transpose(q, pair, 0)
                for half in range(4):
                    if half < 3:
                        index_transpose(q, pair, half + 1)
                    index_pack(q, pair, half)

            def layer0(s, t):
                if t == 0:
                    pe.wait_ge(h_in, 16 * (s + 1))
                pe.wait_ge(agg_made, T * s + t + 3)
                pe.wait_ge(b1_free, b1.next())
                for k in range(KC):
                    nc.tensor.transpose(bank1[:, k * P:(k + 1) * P], h_q[:, t, k * P:(k + 1) * P], ident)
                for k in range(KC):
                    mm = nc.tensor.transpose(bank1[:, (KC + k) * P:(KC + k + 1) * P], agg[:, k * P:(k + 1) * P],
                                             ident)
                mm.then_inc(b1_full, 1)
                pe.wait_ge(b1_free, b1.n + 1)
                pe.wait_ge(b2_free, b2.next())
                for k in range(2 * KC):
                    nc.tensor.matmul(bank2[:, 0:C], cat_t[:, k * P:(k + 1) * P], w0_sb[:, k, :],
                                     start=(k == 0), stop=False)
                nc.tensor.matmul(bank2[:, 0:C], ones_f[0:1, :], b0_row[:, :], start=False, stop=True
                                 ).then_inc(b2_full, 1)

            def project(q, normalised=h2_q, before=lambda: None, after=lambda: None):
                pe.wait_ge(h2_made, T * q + T)
                for k in range(KC):
                    for t in range(T):
                        mm = nc.tensor.transpose(acc[:, k, t * P:(t + 1) * P], normalised[:, t, k * P:(k + 1) * P],
                                             ident)
                mm.then_inc(proj_pe, 1)
                before()
                pe.wait_ge(h2t_made, q + 1)
                pe.wait_ge(b1_free, b1.next())
                for k in range(KC):
                    mm = nc.tensor.matmul(bank1[:, :], wa2_b[:, k, :], h2_t[:, k, :], start=(k == 0),
                                          stop=(k == KC - 1))
                mm.then_inc(b1_full, 1)
                after()
                for t in range(T):
                    for k in range(KC):
                        mm = nc.tensor.matmul(acc[:, t, 0:C + 2], h2_t[:, k, t * P:(t + 1) * P], w1_t[:, k, :],
                                              start=(k == 0), stop=(k == KC - 1))
                mm.then_inc(proj_pe, 1)

            def row_scores(n, diagonals):
                pe.wait_ge(diag_made, n + 1)
                pe.wait_ge(b1_free, b1.next())
                nc.tensor.matmul(bank1[:, :], ones_f[:, :], diagonals, start=True, stop=True).then_inc(b1_full, 1)

            def row_maxima(n):
                pe.wait_ge(m_made, n + 1)
                pe.wait_ge(b1_free, b1.next())
                for t in range(T):
                    mm = nc.tensor.transpose(bank1_b[0:3, t * P:(t + 1) * P], m_c[:, t, :], ident_b[:, :])
                mm.then_inc(b1_full, 1)

            def penalty(g, c, maxima, non_edges):
                for i in range(2):
                    j = 2 * c + i
                    pe.wait_ge(arg_made, 2 * g + i + 1)
                    nc.tensor.matmul(pen[:, i, :], ones_b[:, :], maxima, start=True, stop=False,
                                     skip_group_check=True)
                    for t in range(T):
                        mm = nc.tensor.matmul(pen[:, i, t * P:(t + 1) * P], non_edges[:, t, j * P:(j + 1) * P],
                                              neg_ident[:, :], start=False, stop=(t == T - 1),
                                              skip_group_check=True)
                    mm.then_inc(pen_made, 1)

            def products(a, c, first, last):
                batch = (a % RING) // QB
                for i in range(2):
                    j = 2 * c + i
                    for t in range(T):
                        mm = nc.tensor.matmul(
                            acc[:, t, 0:C + 1], wgt[:, c % 2, i * QR + t * P:i * QR + (t + 1) * P],
                            hid[:, bass.ds(batch * NJ + j, 1), 0:C + 1].rearrange("p a c -> p (a c)"),
                            start=(first and i == 0), stop=(last and i == 1), skip_group_check=True)
                mm.then_inc(wgt_used, 1)

            def attend_setup(a):
                row_scores(a, lin[:, 0, :])
                row_maxima(a)
                pe.wait_ge(b1_free, b1.n + 1)
                penalty(NJ // 2 * a, 0, m_r[:, :], nm_q)

            def chunk(a, c):
                g = NJ // 2 * a + c
                if c + 1 < NJ // 2:
                    penalty(g + 1, c + 1, m_r[:, :], nm_q)
                pe.wait_ge(wgt_made, g + 1)
                if c == 0:
                    pe.wait_ge(out_made, a + 1)
                products(a, c, c == 0, c == NJ // 2 - 1)

            def last_quad():
                setups = LAST - 4

                def task_setup(k):
                    row_scores(setups + k, diag_last)
                    row_maxima(setups + k)

                def task_starts(k):
                    pe.wait_ge(b1_free, b1.n + 1)
                    penalty(TASK_AT[k], TASKS[k][1], m_rows[k % 3], nm_of[TASKS[k][0]])

                project(LAST - 1)
                task_setup(0)
                layer0(LAST, 0)
                task_starts(0)
                for k in range(len(TASKS)):
                    a, first, count = TASKS[k]
                    for c in range(count):
                        g = TASK_AT[k] + c
                        if c + 1 < count:
                            penalty(g + 1, first + c + 1, m_rows[k % 3], nm_of[a])
                        elif k + 1 < len(TASKS) and k != 1:
                            task_starts(k + 1)
                        if (k, c) == (3, 0):
                            task_setup(4)
                        if (k, c) == (5, 0):
                            row_maxima(setups + 6)
                        pe.wait_ge(wgt_made, g + 1)
                        if (k, c) == (0, 0):
                            pe.wait_ge(out_made, LAST - 3)
                        elif (k, c) == (2, 0):
                            pe.wait_ge(hid_made, QUADS)
                        elif c == 0:
                            pe.wait_ge(acc_read, k)
                        products(a, first + c, c == 0, c == count - 1)
                        for n, at in (1, (0, 4)), (3, (2, 2)), (5, (4, 3)), (6, (4, 7)):
                            if (k, c) == at:
                                row_scores(setups + n, diag_last)
                        for n, at in (1, (0, 5)), (3, (2, 3)), (5, (4, 4)):
                            if (k, c) == at:
                                row_maxima(setups + n)
                        if (k, c) in ((0, 1), (0, 6), (1, 2)):
                            layer0(LAST, 1 + ((0, 1), (0, 6), (1, 2)).index((k, c)))
                    if k == 1:
                        pe.wait_ge(acc_read, 2)
                        project(LAST, x_q, lambda: task_setup(2), lambda: task_starts(2))

            def step(s, lo, stages):
                b1.start(s, lo)
                b2.start(s, lo)
                a = s - LAG

                def gathered(t):
                    if "gather" in stages:
                        layer0(s, t)

                if "index" in stages:
                    index_prep(s + 1, 0)
                if "project" in stages:
                    project(s - 1)
                gathered(0)
                if "attend" in stages:
                    attend_setup(a)
                gathered(1)
                if "index" in stages:
                    index_transpose(s + 1, 1, 0)
                for c in range(4):
                    if "attend" in stages:
                        chunk(a, c)
                    if "index" in stages:
                        if c < 3:
                            index_transpose(s + 1, 1, c + 1)
                        index_pack(s + 1, 1, c)
                gathered(2)
                for c in range(4, 8):
                    if "attend" in stages:
                        chunk(a, c)
                gathered(3)

            b1.start(-1, -1)
            b2.start(-1, -1)
            pe.wait_ge(set_act, 1)
            index_prep(0, 0)
            index_prep(0, 1)
            pe.wait_ge(b1_free, b1.n + 1)
            setup_weights()
            schedule(pe, step)
            b1.start(LAST, LAST)
            b2.start(LAST, LAST)
            last_quad()


_INS = ["x", "adj", "L0_gnn_W", "L0_gnn_b", "L1_gnn_W", "L1_gnn_a", "L1_gnn_bias"]


def kernel(**inputs):
    import concourse.bacc as _bacc
    from concourse.bass_utils import run_bass_kernel_spmd as _run

    nc = _bacc.Bacc("TRN2", target_bir_lowering=False, num_devices=1)
    arrays, args = {}, []
    laid_out = [(name, np.ascontiguousarray(inputs[name])) for name in _INS] + [("consts", shape_constants())]
    for name, a in laid_out:
        arrays[f"in_{name}_dram"] = a
        args.append(nc.dram_tensor(f"in_{name}_dram", a.shape, mybir.dt.from_np(a.dtype), kind="ExternalInput").ap())
    out = nc.dram_tensor("out_0_dram", (B, N, C), F32, kind="ExternalOutput").ap()
    table = nc.dram_tensor("table_dram", (ZERO_ROW + 1, C), F32, kind="Internal").ap()
    xmid = nc.dram_tensor("xmid_dram", (ROWS, C), F32, kind="Internal").ap()
    nmask = nc.dram_tensor("nmask_dram", (ROWS, N), BF16, kind="Internal").ap()
    two_layers(nc, *args, out, table, xmid, nmask)
    r = _run(nc, [arrays], core_ids=[0])
    return r.results[0]["out_0_dram"]
```
